# Optimizing a Trainium2 kernel written in Bass

```python
import numpy as np
import jax
import jax.numpy as jnp

def _softmax(x, axis=-1):
    return jax.nn.softmax(x, axis=axis)

def _gelu(x):
    return jax.nn.gelu(x, approximate=True)

def _silu(x):
    return jax.nn.silu(x)

def _sigmoid(x):
    return jax.nn.sigmoid(x)

def _layernorm(x, axis=-1, eps=1e-05):
    m = jnp.mean(x, axis=axis, keepdims=True)
    v = jnp.var(x, axis=axis, keepdims=True)
    return (x - m) / jnp.sqrt(v + eps)

def _scatter_add(tgt, idx, src, axis=0):
    return tgt.at[idx].add(src)

def _segment_sum(src, seg, n):
    return jax.ops.segment_sum(src, seg, n)
kernel_name = 'mk_adj_ffn_d1_adj_r2_d3022d'

def setup_inputs(seed: int=0):
    np.random.seed(seed)
    _w = jnp.asarray

    def _rec_inputs():
        import jax
        import jax.numpy as jnp
        _gk = jax.random.key(seed)
        x = -0.0005207 + 1.001 * jax.random.normal(jax.random.fold_in(_gk, 1), (2048, 128), jnp.float32)
        _w = (1.0 + jnp.arange(2048, dtype=jnp.float32)) ** (-0.5)
        _w = _w / _w.mean()
        _pij = jnp.clip(0.00195312 * _w[:, None] * _w[None, :], 0.0, 1.0)
        _a = jax.random.uniform(jax.random.fold_in(_gk, 2), (2048, 2048)) < _pij
        adj = _a.astype(jnp.int32)
        return (x, adj)
    x, adj = _rec_inputs()

    def _L0_gnn_setup():
        import jax, jax.numpy as jnp
        import numpy as np
        N = 4096
        D_IN = 128
        D_OUT = 128
        NEG_INF = -9000000000000000.0
        key = jax.random.key(seed)
        k1, k2, k3, k4 = jax.random.split(key, 4)
        node_features = jax.random.normal(k1, (N, D_IN), dtype=jnp.float32)
        adjacency_matrix = jax.random.randint(k2, (N, N), 0, 2, dtype=jnp.int32)
        W = jax.random.normal(k3, (D_OUT, D_IN), dtype=jnp.float32) / np.sqrt(D_IN)
        b_W = jnp.zeros((D_OUT,), dtype=jnp.float32)
        a_vec = jax.random.normal(k4, (2 * D_OUT,), dtype=jnp.float32) / np.sqrt(2 * D_OUT)
        b_a = jnp.zeros((1,), dtype=jnp.float32)
        return {'node_features': node_features, 'adjacency_matrix': adjacency_matrix, 'W': W, 'b_W': b_W, 'a_vec': a_vec, 'b_a': b_a}
    _L0_gnn_all = _L0_gnn_setup()
    _L0_gnn_in = {k: v for k, v in _L0_gnn_all.items() if k in ('W', 'b_W', 'a_vec', 'b_a')}
    del _L0_gnn_all

    def _L0_ffn_setup():
        import jax, jax.numpy as jnp
        import numpy as np
        D_IN, D_HID, D_OUT = (128, 256, 128)
        N_EXPERTS, TOP_K = (64, 2)
        B, S = (8, 2048)
        key = jax.random.key(seed)
        ks = jax.random.split(key, 8)
        scale_in = 1.0 / np.sqrt(D_IN)
        scale_hid = 1.0 / np.sqrt(D_HID)
        return {'x': jax.random.normal(ks[0], (B, S, D_IN), dtype=jnp.float32), 'Wr': jax.random.uniform(ks[1], (D_IN, N_EXPERTS), jnp.float32, -scale_in, scale_in), 'br': jax.random.uniform(ks[2], (N_EXPERTS,), jnp.float32, -scale_in, scale_in), 'W1': jax.random.uniform(ks[3], (N_EXPERTS, D_IN, D_HID), jnp.float32, -scale_in, scale_in), 'b1': jax.random.uniform(ks[4], (N_EXPERTS, D_HID), jnp.float32, -scale_in, scale_in), 'W2': jax.random.uniform(ks[5], (N_EXPERTS, D_HID, D_OUT), jnp.float32, -scale_hid, scale_hid), 'b2': jax.random.uniform(ks[6], (N_EXPERTS, D_OUT), jnp.float32, -scale_hid, scale_hid)}
    _L0_ffn_all = _L0_ffn_setup()
    _L0_ffn_in = {k: v for k, v in _L0_ffn_all.items() if k in ('Wr', 'br', 'W1', 'b1', 'W2', 'b2')}
    del _L0_ffn_all
    return {'x': x, 'adj': adj, 'L0_gnn_W': _L0_gnn_in['W'], 'L0_gnn_b_W': _L0_gnn_in['b_W'], 'L0_gnn_a_vec': _L0_gnn_in['a_vec'], 'L0_gnn_b_a': _L0_gnn_in['b_a'], 'L0_ffn_Wr': _L0_ffn_in['Wr'], 'L0_ffn_br': _L0_ffn_in['br'], 'L0_ffn_W1': _L0_ffn_in['W1'], 'L0_ffn_b1': _L0_ffn_in['b1'], 'L0_ffn_W2': _L0_ffn_in['W2'], 'L0_ffn_b2': _L0_ffn_in['b2']}

def reference(x, adj, L0_gnn_W, L0_gnn_b_W, L0_gnn_a_vec, L0_gnn_b_a, L0_ffn_Wr, L0_ffn_br, L0_ffn_W1, L0_ffn_b1, L0_ffn_W2, L0_ffn_b2):
    import jax
    import jax.numpy as jnp

    def _L0_gnn_ref(node_features, adjacency_matrix, W, b_W, a_vec, b_a):
        import jax, jax.numpy as jnp
        import numpy as np
        N = 4096
        D_IN = 128
        D_OUT = 128
        NEG_INF = -9000000000000000.0
        h = node_features @ W.T + b_W
        a1, a2 = (a_vec[:D_OUT], a_vec[D_OUT:])
        e = (h @ a1)[:, None] + (h @ a2)[None, :] + b_a[0]
        e = jnp.where(e > 0, e, 0.2 * e)
        scores = jnp.where(adjacency_matrix > 0, e, jnp.float32(NEG_INF))
        attention = jax.nn.softmax(scores, axis=1)
        h_prime = attention @ h
        return h_prime

    def _L0_ffn_ref(x, Wr, br, W1, b1, W2, b2):
        import jax, jax.numpy as jnp
        import numpy as np
        D_IN, D_HID, D_OUT = (128, 256, 128)
        N_EXPERTS, TOP_K = (64, 2)
        B, S = (8, 2048)
        Bx, Sx, D = x.shape
        xf = x.reshape(-1, D)
        T = xf.shape[0]
        E = Wr.shape[1]
        logits = xf @ Wr + br
        topk_logits, topk_idx = jax.lax.top_k(logits, TOP_K)
        gates = jax.nn.softmax(topk_logits, axis=1)
        combine = jnp.zeros((T, E), xf.dtype).at[jnp.arange(T)[:, None], topk_idx].add(gates)
        out = jnp.zeros((T, W2.shape[-1]), xf.dtype)
        for e in range(E):
            h = jax.nn.relu(xf @ W1[e] + b1[e])
            y = h @ W2[e] + b2[e]
            out = out + combine[:, e:e + 1] * y
        return out.reshape(Bx, Sx, -1)
    x = x + _L0_gnn_ref(_layernorm(x, axis=-1), adj, L0_gnn_W, L0_gnn_b_W, L0_gnn_a_vec, L0_gnn_b_a)
    x = x + _L0_ffn_ref(_layernorm(x, axis=-1)[None], L0_ffn_Wr, L0_ffn_br, L0_ffn_W1, L0_ffn_b1, L0_ffn_W2, L0_ffn_b2)[0]
    return x

_drawn_inputs = setup_inputs


def setup_inputs(seed=0):
    import zlib

    import numpy as np

    out = dict(_drawn_inputs(seed))
    spreads = {'L0_gnn_b_W': (0.0, 0.1)}
    factors = {'L0_ffn_b1': 4.594}
    for name, (base, spread) in spreads.items():
        noise = np.random.default_rng([zlib.crc32(name.encode()), seed]).standard_normal(out[name].shape)
        drawn = base * np.exp(spread * noise) if base else spread * noise
        out[name] = jnp.asarray(drawn.astype(out[name].dtype))
    for name, factor in factors.items():
        out[name] = (out[name] * factor).astype(out[name].dtype)
    return out
```

```python
from contextlib import ExitStack

import concourse.bass as bass
from concourse import mybir


def build(nc, x, adj, w, w_t, b_w, a_vec, b_a, wr, br, w1b, w2, b2, out):
    F32, BF16, I32, U32 = mybir.dt.float32, mybir.dt.bfloat16, mybir.dt.int32, mybir.dt.uint32
    ALU, ACT = mybir.AluOpType, mybir.ActivationFunctionType
    AX = mybir.AxisListType

    P = 128
    N, D = x.shape
    T = N // P
    E = wr.shape[1]
    HID = w2.shape[2] * P
    HB = HID // P
    TOPK = 2
    GRP = 4
    NG = T // GRP
    CB = 4
    W1W = HID + HB
    ROW = D + 2
    ID_COL, GATE_COL = D, D + 1
    MAX_TILES = TOPK * N // P + E - 1
    U = 4
    TILES = -(-MAX_TILES // U) * U
    assert TILES <= P
    EPS = 1e-5
    SLOPE = 0.2
    PENALTY = -(2.0 ** 53)
    SKIP = 1 << 20
    LOWEST = -3.0e38

    ctx = ExitStack()
    with ctx:
        def sb(name, shape, dt=F32):
            return ctx.enter_context(nc.sbuf_tensor(name, shape, dt))

        def sem(name):
            return ctx.enter_context(nc.semaphore(name))

        table = nc.dram_tensor("table", (E * N, ROW), F32, kind="Internal").ap()
        result = nc.dram_tensor("result", (TOPK * N, D), F32, kind="Internal").ap()

        adj_r = sb("adj_r", [P, 4, N], I32)
        z_r = sb("z_r", [P, 3, N])
        pen = sb("pen", [P, N], BF16)
        pt_r = sb("pt_r", [P, 2, T, P])
        trow = sb("trow", [P, N])
        h = sb("h", [P, T, D + 2])
        s8 = sb("s8", [P, T])
        xs = sb("xs", [P, T, D])
        w2s = sb("w2s", [P, E, HB, D])
        store_row = sb("store_row", [P, U], I32)
        rows_out = sb("rows_out", [P, NG, GRP, TOPK, ROW])
        x2T = sb("x2T", [P, GRP * P])
        ident = sb("ident", [P, P])
        before = sb("before", [P, P], BF16)
        upto = sb("upto", [P, P], BF16)
        ones = sb("ones", [P, P], BF16)
        iota_e = sb("iota_e", [P, E])
        iota_i = sb("iota_i", [P, E], I32)
        pidx_i = sb("pidx_i", [P, 1], I32)
        pidx = sb("pidx", [P, 1])
        ids = sb("ids", [P, T, TOPK], I32)
        expo = sb("expo", [P, T])
        w_s = sb("w_s", [P, D])
        wt_s = sb("wt_s", [P, D + 1])
        a_s = sb("a_s", [P, 2])
        a_sum = sb("a_sum", [P, 1])
        a2rep = sb("a2rep", [P, P])
        bwrep = sb("bwrep", [P, P])
        a2w = sb("a2w", [P, P])
        bw_c = sb("bw_c", [P, 1])
        hbias = sb("hbias", [P, D + 1])
        ba_s = sb("ba_s", [P, 1])
        wr_s = sb("wr_s", [P, E])
        br_s = sb("br_s", [P, E])
        b2_s = sb("b2_s", [E, D])
        st = sb("st", [P, T, 6])
        mv = sb("mv", [P, T, 2])
        ve = sb("ve", [P, T])
        rstd = sb("rstd", [P, T])
        st2 = sb("st2", [P, T, 6])
        mv2 = sb("mv2", [P, T, 2])
        ve2 = sb("ve2", [P, T])
        rstd2 = sb("rstd2", [P, T])
        tmax = sb("tmax", [P, T])
        r8 = sb("r8", [P, T])
        v2 = sb("v2", [P, T])
        c_lo = sb("c_lo", [P, T])
        c_hi = sb("c_hi", [P, T])
        rinv = sb("rinv", [P, T])
        lg = sb("lg", [P, GRP, E])
        top8 = sb("top8", [P, GRP, 8])
        idx8 = sb("idx8", [P, GRP, 8], U32)
        idxf = sb("idxf", [P, GRP, TOPK])
        hot = sb("hot", [P, TOPK, GRP, E])
        both = sb("both", [P, T, E], BF16)
        cnt = sb("cnt", [P, NG + 1, E], BF16)
        cnt_t = sb("cnt_t", [P, 2, E], BF16)
        rk = sb("rk", [P, TOPK, GRP, E])
        rank = sb("rank", [P, TOPK, GRP])
        posf = sb("posf", [P, TOPK, GRP])
        pos = sb("pos", [P, NG, TOPK, GRP], I32)
        gd = sb("gd", [P, GRP])
        ge = sb("ge", [P, GRP])
        gs = sb("gs", [P, GRP])
        gate = sb("gate", [P, TOPK, GRP])
        cm = sb("cm", [P, TOPK, GRP, E])
        comb = sb("comb", [P, T, E])
        crow = sb("crow", [P, E])
        ci = sb("ci", [E, 1], I32)
        ci2 = sb("ci2", [E, 1], I32)
        ntf = sb("ntf", [E, 1])
        ntrep = sb("ntrep", [E, P], BF16)
        erow = sb("erow", [P, E])
        strow = sb("strow", [P, E])
        tg = sb("tg", [P, E])
        t_e = sb("t_e", [P, 1])
        t_hot = sb("t_hot", [P, E])
        t_junk = sb("t_junk", [P, 2, E])
        t_c = sb("t_c", [P, 1])
        t_s = sb("t_s", [P, 1])
        t_k = sb("t_k", [P, 1])
        t_last = sb("t_last", [P, 1])
        t_start = sb("t_start", [P, 1])
        t_ec = sb("t_ec", [P, 1])
        t_vals = sb("t_vals", [P, 3])
        z_flat = z_r[:, :, :].rearrange("p s n -> p (s n)")
        ends = [0]

        def carve(width):
            ends.append(ends[-1] + U * width)
            return z_flat[:, ends[-2]:ends[-1]].rearrange("p (u w) -> p u w", u=U)

        w1s = carve(W1W)
        rows_in = carve(ROW)
        xgT = carve(P)
        hT = carve(HB * P).rearrange("p u (b i) -> p u b i", b=HB)
        ys = carve(D)
        rest = z_flat[:, ends[-1]:ends[-1] + 6 * P].rearrange("p (k i) -> p k i", k=6)
        t_rep, etab, skip = rest[:, 0:3, :], rest[:, 3:5, :].bitcast(I32), rest[:, 5, :]
        xh = z_r[:, 0, :].rearrange("p (t d) -> p t d", t=T)
        xhT = z_r[:, 1, :]
        fill = z_r[:, 2, 0:ROW]
        combT = adj_r[0:E, 2, :].bitcast(F32)
        zl = adj_r[:, 0:2, :].bitcast(F32).rearrange("p k (t d) -> p k t d", t=T)

        bank = [ctx.enter_context(nc.psum_tensor(f"bank{i}", [P, 512], F32)) for i in range(8)]
        OB, M0, M1 = bank[4:6], bank[6], bank[7]

        d_x = [sem(f"d_x{i}") for i in range(4)]
        d_small = sem("d_small")
        d_br = sem("d_br")
        d_w2 = sem("d_w2")
        d_adj = [sem(f"d_adj{i}") for i in range(4)]
        d_fill = sem("d_fill")
        d_put = sem("d_put")
        s_const = sem("s_const")
        s_pool = sem("s_pool")
        s_fill = sem("s_fill")
        s_prep = sem("s_prep")
        s_stat = sem("s_stat")
        s_rstd = sem("s_rstd")
        s_norm = sem("s_norm")
        s_xT = sem("s_xT")
        s_xTs = sem("s_xTs")
        s_wa = sem("s_wa")
        s_was = sem("s_was")
        s_tr = sem("s_tr")
        s_trs = sem("s_trs")
        s_h = sem("s_h")
        s_hs = sem("s_hs")
        s_pen = sem("s_pen")
        s_z = sem("s_z")
        s_s8 = sem("s_s8")
        s_rv = sem("s_rv")
        s_lo = sem("s_lo")
        s_hi = sem("s_hi")
        s_low = sem("s_low")
        s_lk = sem("s_lk")
        s_pt = sem("s_pt")
        s_ea = sem("s_ea")
        s_o = sem("s_o")
        s_ri = sem("s_ri")
        s_x1 = sem("s_x1")
        s_st2 = sem("s_st2")
        s_mv2 = sem("s_mv2")
        s_ve2 = sem("s_ve2")
        s_rstd2 = sem("s_rstd2")
        s_row = sem("s_row")
        s_x2t = sem("s_x2t")
        s_x2s = sem("s_x2s")
        s_lgp = sem("s_lgp")
        s_lg = sem("s_lg")
        s_dve = sem("s_dve")
        s_gd = sem("s_gd")
        s_ge = sem("s_ge")
        s_gate = sem("s_gate")
        s_hot = sem("s_hot")
        s_both = sem("s_both")
        s_cnt = sem("s_cnt")
        s_rk = sem("s_rk")
        s_pos = sem("s_pos")
        s_comb = sem("s_comb")
        s_pl = sem("s_pl")
        s_ct = sem("s_ct")
        s_cts = sem("s_cts")
        s_b2 = sem("s_b2")
        s_base = sem("s_base")
        s_tp = sem("s_tp")
        s_tt = sem("s_tt")
        s_tab = sem("s_tab")
        e_w = [sem(f"e_w{i}") for i in range(U)]
        e_r = [sem(f"e_r{i}") for i in range(U)]
        e_put = [sem(f"e_put{i}") for i in range(U)]
        e_xt = sem("e_xt")
        e_xts = sem("e_xts")
        e_h = sem("e_h")
        e_ha = sem("e_ha")
        e_hb = sem("e_hb")
        e_y = sem("e_y")
        e_ys = sem("e_ys")
        e_id = sem("e_id")
        d_z = [sem(f"d_z{i}") for i in range(4)]
        s_f1 = sem("s_f1")
        s_f2 = sem("s_f2")
        d_out = sem("d_out")

        SMALL = 9 * 16
        block = ctx.enter_context(nc.Block())

        def xp(u):
            return bank[u % 2][:, 0:P]

        def hp(u, b):
            return bank[2 + 2 * b + u % 2][:, 0:P]

        def yp(u):
            return bank[6 + u % 2][:, 0:D]

        def low(t):
            return adj_r[:, t % 4, :].bitcast(F32)

        @block.sync
        def _(sp):
            xt = x.rearrange("(t p) d -> p t d", p=P)
            sp.dma_start(xs[:, 0:4, :], xt[:, 0:4, :]).then_inc(d_x[0], 16)
            sp.dma_start(adj_r[:, 0, :], adj[0:P, :]).then_inc(d_adj[0], 16)
            for c in range(1, 4):
                sp.dma_start(xs[:, 4 * c:4 * c + 4, :], xt[:, 4 * c:4 * c + 4, :]).then_inc(d_x[c], 16)
            for t in range(1, T):
                if t >= 4:
                    sp.wait_ge(s_lk, t - 3)
                sp.dma_start(adj_r[:, t % 4, :], adj[t * P:(t + 1) * P, :]).then_inc(d_adj[t % 4], 16)
                if t == 4:
                    sp.wait_ge(s_fill, 3)
                    sp.dma_start(table.rearrange("(e n) w -> n e w", e=E)[0:P, :, :],
                                 fill.rearrange("p (e w) -> p e w", e=1).to_broadcast([P, E, ROW])
                                 ).then_inc(d_fill, 16)
            sp.dma_start(w2s[:, :, :, :], w2).then_inc(d_w2, 16)

            sp.wait_ge(s_tab, 3)
            for u in range(U):
                if u == 0:
                    sp.wait_ge(d_put, 16 * TOPK * T)
                e = sp.value_load(etab[0:1, 0, u:u + 1], min_val=0, max_val=E - 1)
                r = sp.value_load(etab[0:1, 1, u:u + 1], min_val=0, max_val=E * N - P)
                sp.dma_start(rows_in[:, u, :], table[bass.ds(r, P), :]).then_inc(e_r[u], 16)
                sp.dma_start(w1s[:, u, :], w1b[bass.ds(e, 1), :, :].rearrange("e p w -> p (e w)")).then_inc(e_w[u], 16)
            with sp.Fori(1, TILES // U) as i:
                for u in range(U):
                    e = sp.value_load(etab[0:1, 0, bass.ds(i * U + u, 1)], min_val=0, max_val=E - 1)
                    r = sp.value_load(etab[0:1, 1, bass.ds(i * U + u, 1)], min_val=0, max_val=E * N - P)
                    sp.wait_ge(e_put[u], i * 16)
                    sp.dma_start(rows_in[:, u, :], table[bass.ds(r, P), :]).then_inc(e_r[u], 16)
                    sp.dma_start(w1s[:, u, :], w1b[bass.ds(e, 1), :, :].rearrange("e p w -> p (e w)")).then_inc(e_w[u], 16)

            for u in range(U):
                sp.wait_ge(e_put[u], 16 * (TILES // U))
            zt = result.rearrange("(k t p) d -> p k t d", k=TOPK, p=P)
            for c in range(4):
                for k in range(TOPK):
                    sp.dma_start(zl[:, k, 4 * c:4 * c + 4, :], zt[:, k, 4 * c:4 * c + 4, :]).then_inc(d_z[c], 16)
            ot = out.rearrange("(t p) d -> p t d", p=P)
            for c in range(4):
                sp.wait_ge(s_f2, c + 1)
                sp.dma_start(ot[:, 4 * c:4 * c + 4, :], xs[:, 4 * c:4 * c + 4, :]).then_inc(d_out, 16)
            sp.wait_ge(d_out, 64)

        @block.gpsimd
        def _(pool):
            def link(ins, n=[0]):
                n[0] += 1
                ins.then_inc(s_pl, 1)
                pool.wait_ge(s_pl, n[0])

            pool.memset(expo[:, :], -0.5)
            link(pool.memset(ident[:, :], 0.0))
            pool.affine_select(out=ident[:, :], in_=ident[:, :], compare_op=ALU.not_equal, fill=1.0,
                               base=0, pattern=[[-1, P]], channel_multiplier=1).then_inc(s_const, 1)
            pool.memset(fill, 0.0).then_inc(s_fill, 1)
            pool.wait_ge(s_fill, 1)
            pool.memset(fill[:, ID_COL:ID_COL + 1].bitcast(I32), SKIP).then_inc(s_fill, 2)
            pool.memset(h[:, :, D + 1:D + 2], 1.0).then_inc(s_pool, 1)
            link(pool.memset(ones[:, :], 1.0))
            pool.affine_select(out=before[:, :], in_=ones[:, :], compare_op=ALU.is_gt, fill=0.0,
                               base=0, pattern=[[1, P]], channel_multiplier=-1).then_inc(s_pool, 1)
            pool.affine_select(out=upto[:, :], in_=ones[:, :], compare_op=ALU.is_ge, fill=0.0,
                               base=0, pattern=[[1, P]], channel_multiplier=-1).then_inc(s_pool, 1)
            pool.iota(iota_i[:, :], pattern=[[1, E]], base=0, channel_multiplier=0)
            pool.iota(ids[:, :, :], pattern=[[P, T], [N, TOPK]], base=0, channel_multiplier=1)
            link(pool.iota(pidx_i[:, :], pattern=[[1, 1]], base=0, channel_multiplier=1))
            pool.tensor_copy(iota_e[:, :], iota_i[:, :])
            pool.tensor_copy(pidx[:, :], pidx_i[:, :])
            pool.memset(cnt[:, 0, :], 0.0).then_inc(s_pool, 1)
            pool.wait_ge(s_stat, 1)
            pool.tensor_tensor(rstd[:, :], ve[:, :], expo[:, :], ALU.pow).then_inc(s_rstd, 1)

            def rstd_of(t):
                pool.wait_ge(s_mv2, t + 1)
                pool.tensor_scalar(ve2[:, t:t + 1], mv2[:, t, 1:2], EPS, None, ALU.add).then_inc(s_ve2, 1)
                pool.wait_ge(s_ve2, t + 1)
                pool.tensor_tensor(rstd2[:, t:t + 1], ve2[:, t:t + 1], expo[:, 0:1], ALU.pow).then_inc(s_rstd2, 1)

            def counts(q):
                pool.wait_ge(s_both, q + 1)
                b = both[:, q * GRP:(q + 1) * GRP, :]
                link(pool.tensor_tensor(cnt_t[:, :, :], b[:, 0:2, :], b[:, 2:4, :], ALU.add))
                link(pool.tensor_tensor(cnt_t[:, 0, :], cnt_t[:, 0, :], cnt_t[:, 1, :], ALU.add))
                pool.tensor_tensor(cnt[:, q + 1, :], cnt[:, q, :], cnt_t[:, 0, :], ALU.add).then_inc(s_cnt, 1)

            def place(t):
                q, g = t // GRP, t % GRP
                pool.wait_ge(s_pos, q + 1)
                for k in range(TOPK):
                    pool.indirect_dma_start(table[:, :], bass.IndirectOffsetOnAxis(pos[:, q, k, g:g + 1], 0),
                                            rows_out[:, q, g, k, :], None).then_inc(d_put, 16)

            def combine(q):
                pool.wait_ge(s_gate, q + 1)
                for k in range(TOPK):
                    ins = pool.tensor_tensor(cm[:, k, :, :], hot[:, k, :, :],
                                             gate[:, k, :].rearrange("p (g e) -> p g e", e=1).to_broadcast([P, GRP, E]), ALU.mult)
                link(ins)
                pool.tensor_tensor(comb[:, GRP * q:GRP * q + GRP, :], cm[:, 0, :, :], cm[:, 1, :, :], ALU.add).then_inc(s_comb, 1)

            for s in range(3, T + 12):
                if 0 <= s - 3 < T:
                    rstd_of(s - 3)
                if s == 12:
                    pool.wait_ge(d_fill, 16)
                for q in range(NG):
                    if s == GRP * q + 10:
                        counts(q)
                    if s == GRP * q + 12:
                        place(GRP * q)
                        combine(q)
                    if GRP * q + 12 < s < GRP * q + 12 + GRP:
                        place(s - 12)

            limit = pool.alloc_register("last_result_row")
            pool.reg_mov(limit, TOPK * N - 1)
            for u in range(U):
                pool.wait_ge(e_ys, u + 1)
                pool.wait_ge(e_id, u + 1)
                pool.indirect_dma_start(result[:, :], bass.IndirectOffsetOnAxis(store_row[:, u:u + 1], 0),
                                        ys[:, u, :], None, bounds_check=limit, oob_is_err=False).then_inc(e_put[u], 16)
            tile = pool.alloc_register("tiles_stored")
            pool.reg_mov(tile, U + 1)
            with pool.Fori(1, TILES // U) as i:
                for u in range(U):
                    pool.wait_ge(e_ys, tile)
                    pool.wait_ge(e_id, tile)
                    pool.reg_add(tile, tile, 1)
                    pool.indirect_dma_start(result[:, :], bass.IndirectOffsetOnAxis(store_row[:, u:u + 1], 0),
                                            ys[:, u, :], None, bounds_check=limit, oob_is_err=False).then_inc(e_put[u], 16)

        @block.scalar
        def _(act):
            for dst, src in ((w_s[:, :], w), (wt_s[:, 0:D], w_t),
                             (a_s[:, :], a_vec),
                             (bw_c[:, :], b_w.rearrange("(p o) -> p o", o=1)),
                             (hbias[:, 0:D], b_w.rearrange("(o d) -> o d", o=1).to_broadcast([P, D])),
                             (ba_s[:, :], b_a.rearrange("(o d) -> o d", o=1).to_broadcast([P, 1])),
                             (wr_s[:, :], wr),
                             (br_s[:, :], br.rearrange("(o d) -> o d", o=1).to_broadcast([P, E])),
                             (b2_s[:, :], b2)):
                act.dma_start(dst, src).then_inc(d_small, 16)
            for b in range(4):
                act.wait_ge(s_xT, b + 1)
                act.activation(xhT[:, 512 * b:512 * b + 512], bank[b][:, :], ACT.Copy).then_inc(s_xTs, 1)
            for b in range(4):
                act.wait_ge(s_tr, b + 1)
                act.activation(trow[:, 512 * b:512 * b + 512], bank[b][:, :], ACT.Copy).then_inc(s_trs, 1)

            def scores(t):
                if t == 0:
                    act.wait_ge(s_s8, 1)
                act.wait_ge(s_z, t + 1)
                act.activation(r8[:, t:t + 1], tmax[:, t:t + 1], ACT.Relu, bias=s8[:, t:t + 1], scale=1.0 - SLOPE).then_inc(s_rv, 1)
                act.activation(v2[:, t:t + 1], tmax[:, t:t + 1], ACT.Copy, scale=-SLOPE).then_inc(s_rv, 1)
                act.wait_ge(s_rv, 2 * (t + 1))
                act.activation(c_lo[:, t:t + 1], r8[:, t:t + 1], ACT.Identity, bias=v2[:, t:t + 1], scale=-1.0).then_inc(s_lo, 1)
                act.wait_ge(s_lo, t + 1)
                act.activation(low(t), z_r[:, t % 3, :], ACT.Identity, bias=c_lo[:, t:t + 1], scale=SLOPE).then_inc(s_low, 1)
                act.activation(c_hi[:, t:t + 1], c_lo[:, t:t + 1], ACT.Identity, bias=s8[:, t:t + 1]).then_inc(s_hi, 1)

            def evac(t):
                for b in range(4):
                    act.wait_ge(s_pt, 4 * t + b + 1)
                    if t >= 2:
                        act.wait_ge(s_o, t - 1)
                    act.activation(pt_r[:, t % 2, CB * b:CB * b + CB, :].rearrange("p c i -> p (c i)"),
                                   bank[b][:, :], ACT.Exp).then_inc(s_ea, 1)

            def route_a(q):
                act.wait_ge(s_x2t, q + 1)
                act.activation(x2T[:, :], M0[:, :], ACT.Copy).then_inc(s_x2s, 1)

            def route_b(q):
                act.wait_ge(s_gd, q + 1)
                act.activation(ge[:, :], gd[:, :], ACT.Exp).then_inc(s_ge, 1)

            def route_c(q):
                act.wait_ge(s_ct, q + 1)
                act.activation(combT[:, GRP * P * q:GRP * P * (q + 1)], bank[q][0:E, :], ACT.Copy).then_inc(s_cts, 1)

            for s in range(T + 9):
                if s < T:
                    scores(s)
                if 1 <= s <= T:
                    evac(s - 1)
                for q in range(NG):
                    if s == GRP * q + 9:
                        route_a(q)
                    if s == GRP * q + 11:
                        route_b(q)
            for q in range(NG):
                route_c(q)

            def relu(u, n):
                act.wait_ge(e_h, n)
                act.activation(hT[:, u, 0, :], hp(u, 0), ACT.Relu, bias=w1s[:, u, HID:HID + 1]).then_inc(e_ha, 1)

            def weigh(u, n):
                act.wait_ge(e_y, n)
                act.activation(ys[:, u, :], yp(u), ACT.Copy, scale=rows_in[:, u, GATE_COL:GATE_COL + 1]).then_inc(e_ys, 1)

            for u in range(U):
                relu(u, u + 1)
                if u:
                    weigh(u - 1, u)
            with act.Fori(1, TILES // U) as i:
                for u in range(U):
                    relu(u, i * U + (u + 1))
                    weigh((u - 1) % U, i * U + u)
            weigh(U - 1, TILES)

        @block.vector
        def _(dve):
            chain = [0]

            def link(ins):
                chain[0] += 1
                ins.then_inc(s_dve, 1)
                dve.wait_ge(s_dve, chain[0])

            dve.wait_ge(d_small, SMALL)
            dve.tensor_copy(a2rep[:, :], a_s[:, 1:2].to_broadcast([P, P]))
            dve.tensor_copy(bwrep[:, :], bw_c[:, 0:1].to_broadcast([P, P]))
            dve.tensor_tensor(a_sum[:, :], a_s[:, 0:1], a_s[:, 1:2], ALU.add).then_inc(s_prep, 1)
            for t in range(T):
                if t % 4 == 0:
                    dve.wait_ge(d_x[t // 4], 16)
                ins = dve.bn_stats(st[:, t, :], xs[:, t, :])
            link(ins)
            for t in range(T):
                ins = dve.bn_aggr(mv[:, t, :], st[:, t, :])
            link(ins)
            dve.tensor_scalar(ve[:, :], mv[:, :, 1], EPS, None, ALU.add).then_inc(s_stat, 1)
            dve.wait_ge(s_wa, 1)
            dve.tensor_copy(a2w[:, :], bank[4][:, 0:P])
            dve.tensor_copy(wt_s[:, D:D + 1], bank[5][:, 0:1])
            dve.tensor_tensor(hbias[:, D:D + 1], bank[6][:, 0:1], ba_s[:, :], ALU.add).then_inc(s_was, 1)
            dve.wait_ge(s_rstd, 1)
            dve.wait_ge(s_fill, 3)
            for t in range(T):
                ins = dve.tensor_scalar(xh[:, t, :], xs[:, t, :], mv[:, t, 0:1], rstd[:, t:t + 1], ALU.subtract, ALU.mult)
                if t % 4 == 3:
                    ins.then_inc(s_norm, 1)

            def h_evac(c):
                dve.wait_ge(s_h, c + 1)
                dve.tensor_tensor(h[:, 2 * c:2 * c + 2, 0:D + 1],
                                  bank[(c + 4) % 8][:, 0:2 * (D + 1)].rearrange("p (t d) -> p t d", t=2),
                                  hbias[:, :].rearrange("p (t d) -> p t d", t=1).to_broadcast([P, 2, D + 1]),
                                  ALU.add).then_inc(s_hs, 1)

            def penalty(t):
                dve.wait_ge(d_adj[t % 4], 16 * (t // 4 + 1))
                if t >= 1:
                    dve.wait_ge(s_z, t)
                dve.tensor_scalar(pen[:, :], adj_r[:, t % 4, :], 0, PENALTY, ALU.is_le, ALU.mult).then_inc(s_pen, 1)

            def scores(t):
                if t == 0:
                    dve.wait_ge(s_trs, 4)
                    dve.wait_ge(s_h, 8)
                if t == 2:
                    dve.wait_ge(d_fill, 16)
                if t >= 3:
                    dve.wait_ge(s_pt, 4 * (t - 2))
                dve.wait_ge(s_pen, t + 1)
                dve.tensor_tensor_reduce(out=z_r[:, t % 3, :], in0=pen[:, :], in1=trow[:, :], scale=1.0,
                                         scalar=LOWEST, op0=ALU.add, op1=ALU.max, accum_out=tmax[:, t:t + 1]).then_inc(s_z, 1)

            def leaky(t):
                dve.wait_ge(s_low, t + 1)
                dve.wait_ge(s_hi, t + 1)
                z = z_r[:, t % 3, :]
                dve.scalar_tensor_tensor(z, z, c_hi[:, t:t + 1], low(t), ALU.add, ALU.max).then_inc(s_lk, 1)

            def residual(t):
                dve.wait_ge(s_o, t + 1)
                dve.reciprocal(rinv[:, t:t + 1], OB[t % 2][:, D + 1:D + 2]).then_inc(s_ri, 1)
                dve.wait_ge(s_ri, t + 1)
                dve.scalar_tensor_tensor(xs[:, t, :], OB[t % 2][:, 0:D], rinv[:, t:t + 1], xs[:, t, :],
                                         ALU.mult, ALU.add).then_inc(s_x1, 1)
                dve.wait_ge(s_x1, t + 1)
                dve.bn_stats(st2[:, t, :], xs[:, t, :]).then_inc(s_st2, 1)
                dve.wait_ge(s_st2, t + 1)
                dve.bn_aggr(mv2[:, t, :], st2[:, t, :]).then_inc(s_mv2, 1)

            def norm(t):
                q, g = t // GRP, t % GRP
                dve.wait_ge(s_rstd2, t + 1)
                if g == 0 and q == 0:
                    dve.wait_ge(s_pool, 4)
                dve.tensor_scalar(rows_out[:, q, g, :, 0:D],
                                  xs[:, t, :].rearrange("p (k d) -> p k d", k=1).to_broadcast([P, TOPK, D]),
                                  mv2[:, t, 0:1], rstd2[:, t:t + 1], ALU.subtract, ALU.mult).then_inc(s_row, 1)

            def top2(q):
                dve.wait_ge(s_lgp, q + 1)
                link(dve.tensor_tensor(lg[:, :, :], M1[:, 0:GRP * E].rearrange("p (g e) -> p g e", g=GRP),
                                       br_s[:, :].rearrange("p (g e) -> p g e", g=1).to_broadcast([P, GRP, E]), ALU.add))
                for g in range(GRP):
                    ins = dve.max(top8[:, g, :], lg[:, g, :])
                link(ins)
                dve.tensor_tensor(gd[:, :], top8[:, :, 1], top8[:, :, 0], ALU.subtract).then_inc(s_gd, 1)
                for g in range(GRP):
                    ins = dve.max_index(idx8[:, g, :], top8[:, g, :], lg[:, g, :])
                link(ins)
                link(dve.tensor_copy(idxf[:, :, :], idx8[:, :, 0:TOPK]))
                if q >= 1:
                    dve.wait_ge(s_comb, q)
                for k in range(TOPK):
                    ins = dve.tensor_tensor(hot[:, k, :, :],
                                            iota_e[:, :].rearrange("p (g e) -> p g e", g=1).to_broadcast([P, GRP, E]),
                                            idxf[:, :, k:k + 1].to_broadcast([P, GRP, E]), ALU.is_equal)
                link(ins)
                dve.tensor_tensor(both[:, q * GRP:(q + 1) * GRP, :], hot[:, 0, :, :], hot[:, 1, :, :], ALU.add).then_inc(s_both, 1)

            def place(q):
                dve.wait_ge(s_ge, q + 1)
                link(dve.tensor_scalar(gs[:, :], ge[:, :], 1.0, None, ALU.add))
                link(dve.reciprocal(gate[:, 0, :], gs[:, :]))
                dve.tensor_tensor(gate[:, 1, :], ge[:, :], gate[:, 0, :], ALU.mult).then_inc(s_gate, 1)
                dve.wait_ge(s_rk, q + 1)
                for k in range(TOPK):
                    ins = dve.tensor_tensor(rk[:, k, :, :], M1[:, 256:256 + GRP * E].rearrange("p (g e) -> p g e", g=GRP),
                                            hot[:, k, :, :], ALU.mult)
                link(ins)
                link(dve.tensor_reduce(rank[:, :, :], rk[:, :, :, :], AX.X, ALU.add))
                link(dve.scalar_tensor_tensor(posf[:, :, :], idxf[:, :, :].rearrange("p g k -> p k g"), float(N),
                                              rank[:, :, :], ALU.mult, ALU.add))
                dve.wait_ge(s_gate, q + 1)
                dve.tensor_copy(rows_out[:, q, :, :, ID_COL].bitcast(I32), ids[:, GRP * q:GRP * q + GRP, :])
                dve.tensor_copy(rows_out[:, q, :, :, GATE_COL], gate[:, :, :].rearrange("p k g -> p g k"))
                dve.tensor_copy(pos[:, q, :, :], posf[:, :, :]).then_inc(s_pos, 1)

            def base(q):
                dve.wait_ge(s_b2, q + 1)
                xq = xs[:, GRP * q:GRP * q + GRP, :].rearrange("p g d -> p (g d)")
                dve.tensor_tensor(xq, xq, bank[q][:, :], ALU.add).then_inc(s_base, 1)

            penalty(0)
            for c in range(8):
                h_evac(c)
            dve.wait_ge(s_hs, 8)
            dve.tensor_scalar(s8[:, :], h[:, :, D], 1.0 - SLOPE, None, ALU.mult).then_inc(s_s8, 1)
            for s in range(T + 9):
                if s < T:
                    if s >= 1:
                        penalty(s)
                    scores(s)
                if 1 <= s <= T:
                    leaky(s - 1)
                if 0 <= s - 4 < T:
                    norm(s - 4)
                if 0 <= s - 3 < T:
                    residual(s - 3)
                for q in range(NG):
                    if s == GRP * q + 10:
                        top2(q)
                    if s == GRP * q + 12:
                        place(q)

            dve.wait_ge(s_tp, 1)
            link(dve.tensor_scalar(ci[:, :], M1[0:E, 0:1], float(P - 1), None, ALU.add))
            dve.tensor_copy(crow[:, :], M1[:, E:2 * E])
            link(dve.tensor_scalar(ci2[:, :], ci[:, :], P.bit_length() - 1, None, ALU.arith_shift_right))
            link(dve.tensor_copy(ntf[:, :], ci2[:, :]))
            dve.tensor_copy(ntrep[:, :], ntf[:, :].to_broadcast([E, P])).then_inc(s_tt, 1)
            dve.wait_ge(s_tp, 2)
            link(dve.tensor_copy(strow[:, :], M1[:, 3 * E:4 * E]))
            link(dve.tensor_scalar(tg[:, :], M1[:, 2 * E:3 * E], pidx[:, :], None, ALU.is_le))
            link(dve.tensor_reduce(t_e[:, :], tg[:, :], AX.X, ALU.add))
            link(dve.tensor_scalar(t_hot[:, :], iota_e[:, :], t_e[:, :], None, ALU.is_equal))
            dve.tensor_tensor(t_junk[:, 0, :], t_hot[:, :], crow[:, :], ALU.mult)
            link(dve.tensor_tensor(t_junk[:, 1, :], t_hot[:, :], strow[:, :], ALU.mult))
            dve.tensor_reduce(t_c[:, :], t_junk[:, 0, :], AX.X, ALU.add)
            link(dve.tensor_reduce(t_s[:, :], t_junk[:, 1, :], AX.X, ALU.add))
            dve.tensor_scalar(t_last[:, :], t_c[:, :], float(-P), 0.0, ALU.add, ALU.max)
            link(dve.tensor_tensor(t_k[:, :], pidx[:, :], t_s[:, :], ALU.subtract))
            link(dve.tensor_scalar(t_k[:, :], t_k[:, :], float(P), None, ALU.mult))
            dve.tensor_scalar(t_ec[:, :], t_e[:, :], float(E - 1), None, ALU.min)
            link(dve.tensor_tensor(t_start[:, :], t_k[:, :], t_last[:, :], ALU.min))
            dve.tensor_copy(t_vals[:, 0:1], t_ec[:, :])
            dve.scalar_tensor_tensor(t_vals[:, 1:2], t_ec[:, :], float(N), t_start[:, :], ALU.mult, ALU.add)
            link(dve.tensor_tensor(t_vals[:, 2:3], t_k[:, :], t_start[:, :], ALU.subtract))
            dve.tensor_copy(t_rep[:, :, :], t_vals[:, :].rearrange("p (k o) -> p k o", o=1).to_broadcast([P, 3, P])).then_inc(s_tt, 1)
            for q in range(NG):
                base(q)
            dve.wait_ge(s_tp, 3)
            dve.tensor_copy(etab[:, :, :], M1[:, 0:2 * P].rearrange("p (k o) -> p k o", k=2)).then_inc(s_tab, 1)
            dve.tensor_scalar(skip[:, :], M1[:, 2 * P:3 * P], pidx[:, :], float(SKIP), ALU.is_gt, ALU.mult).then_inc(s_tab, 2)

            def take(u, n, t):
                dve.wait_ge(e_xt, n)
                dve.tensor_copy(xgT[:, u, :], xp(u)).then_inc(e_xts, 1)
                dve.tensor_tensor(store_row[:, u:u + 1], rows_in[:, u, ID_COL:ID_COL + 1].bitcast(I32), skip[:, t],
                                  ALU.add).then_inc(e_id, 1)

            def relu(u, n):
                dve.wait_ge(e_h, n)
                dve.tensor_scalar(hT[:, u, 1, :], hp(u, 1), w1s[:, u, HID + 1:HID + 2], 0.0, ALU.add, ALU.max).then_inc(e_hb, 1)

            dve.wait_ge(s_tab, 3)
            for u in range(U):
                take(u, u + 1, slice(u, u + 1))
                if u:
                    relu(u - 1, u)
            with dve.Fori(1, TILES // U) as i:
                for u in range(U):
                    take(u, i * U + (u + 1), bass.ds(i * U + u, 1))
                    relu((u - 1) % U, i * U + u)
            relu(U - 1, TILES)

            for c in range(4):
                dve.wait_ge(d_z[c], 32)
                xc = xs[:, 4 * c:4 * c + 4, :]
                dve.tensor_tensor(xc, xc, zl[:, 0, 4 * c:4 * c + 4, :], ALU.add).then_inc(s_f1, 1)
                dve.wait_ge(s_f1, c + 1)
                dve.tensor_tensor(xc, xc, zl[:, 1, 4 * c:4 * c + 4, :], ALU.add).then_inc(s_f2, 1)

        @block.tensor
        def _(pe):
            pe.wait_ge(s_prep, 1)
            pe.matmul(bank[4][:, 0:P], w_s[:, :], a2rep[:, :], start=True, stop=True)
            pe.matmul(bank[5][:, 0:1], w_s[:, :], a_s[:, 0:1], start=True, stop=True)
            pe.matmul(bank[6][:, 0:1], bwrep[:, :], a_sum[:, :], start=True, stop=True).then_inc(s_wa, 1)
            pe.wait_ge(s_const, 1)
            for b in range(4):
                pe.wait_ge(s_norm, b + 1)
                for c in range(CB):
                    ins = pe.transpose(bank[b][:, P * c:P * c + P], xh[:, CB * b + c, :], ident[:, :])
                ins.then_inc(s_xT, 1)
            pe.wait_ge(s_was, 1)
            for b in range(4):
                pe.wait_ge(s_xTs, b + 1)
                pe.matmul(bank[b][:, :], a2w[:, :], xhT[:, 512 * b:512 * b + 512], start=True, stop=True).then_inc(s_tr, 1)
            for c in range(8):
                if c >= 4:
                    pe.wait_ge(s_trs, c - 3)
                for j in range(2):
                    t = 2 * c + j
                    ins = pe.matmul(bank[(c + 4) % 8][:, j * (D + 1):(j + 1) * (D + 1)], xhT[:, P * t:P * t + P],
                                    wt_s[:, :], start=True, stop=True)
                ins.then_inc(s_h, 1)

            def turn(t):
                pe.wait_ge(s_lk, t + 1)
                for b in range(4):
                    if t == 0:
                        pe.wait_ge(s_hs, 8)
                    else:
                        pe.wait_ge(s_ea, 4 * (t - 1) + b + 1)
                    for c in range(CB):
                        j = CB * b + c
                        ins = pe.transpose(bank[b][:, P * c:P * c + P], z_r[:, t % 3, P * j:P * j + P], ident[:, :])
                    ins.then_inc(s_pt, 1)

            def attend(t):
                if t >= 2:
                    pe.wait_ge(s_x1, t - 1)
                for j in range(T):
                    b = j // CB
                    if j % CB == 0:
                        pe.wait_ge(s_ea, 4 * t + b + 1)
                    ins = pe.matmul(OB[t % 2][:, 0:D + 2], pt_r[:, t % 2, j, :], h[:, j, :], start=(j == 0), stop=(j == T - 1))
                ins.then_inc(s_o, 1)

            def route_a(q):
                pe.wait_ge(s_row, GRP * (q + 1))
                if q >= 1:
                    pe.wait_ge(s_x2s, q)
                for g in range(GRP):
                    ins = pe.transpose(M0[:, P * g:P * g + P], rows_out[:, q, g, 0, 0:D], ident[:, :])
                ins.then_inc(s_x2t, 1)

            def route_b(q):
                pe.wait_ge(s_x2s, q + 1)
                if q >= 1:
                    pe.wait_ge(s_pos, q)
                for g in range(GRP):
                    ins = pe.matmul(M1[:, E * g:E * g + E], x2T[:, P * g:P * g + P], wr_s[:, :], start=True, stop=True)
                ins.then_inc(s_lgp, 1)

            def route_c(q):
                pe.wait_ge(s_both, q + 1)
                if q >= 1:
                    pe.wait_ge(s_cnt, q)
                    pe.wait_ge(s_pos, q)
                for g in range(GRP):
                    rows = [(before, both[:, GRP * q + g, :]), (ones, cnt[:, q, :])] + [(ones, both[:, GRP * q + j, :]) for j in range(g)]
                    for n, (lt, r) in enumerate(rows):
                        ins = pe.matmul(M1[:, 256 + E * g:256 + E * g + E], lt[:, :], r, start=(n == 0), stop=(n == len(rows) - 1))
                ins.then_inc(s_rk, 1)

            def route_d(q):
                pe.wait_ge(s_comb, q + 1)
                for g in range(GRP):
                    ins = pe.transpose(bank[q][0:E, P * g:P * g + P], comb[:, GRP * q + g, :], ident[:, :])
                ins.then_inc(s_ct, 1)

            def route_e(q):
                pe.wait_ge(s_cts, q + 1)
                for g in range(GRP):
                    ins = pe.matmul(bank[q][:, P * g:P * g + P], combT[:, P * (GRP * q + g):P * (GRP * q + g + 1)], b2_s[:, :], start=True, stop=True)
                ins.then_inc(s_b2, 1)

            for s in range(T + 9):
                if s < T:
                    turn(s)
                if 1 <= s <= T:
                    attend(s - 1)
                for q in range(NG):
                    if s == GRP * q + 8:
                        route_a(q)
                    if s == GRP * q + 9:
                        route_b(q)
                    if s == GRP * q + 10:
                        route_c(q)

            pe.wait_ge(s_cnt, NG)
            pe.wait_ge(s_pos, NG)
            total = cnt[:, NG, :]
            pe.matmul(M1[0:E, 0:1], total, ones[:, 0:1], start=True, stop=True)
            pe.matmul(M1[:, E:2 * E], ones[:, :], total, start=True, stop=True).then_inc(s_tp, 1)
            for q in range(NG):
                route_d(q)
            pe.wait_ge(s_tt, 1)
            pe.matmul(M1[:, 2 * E:3 * E], ntrep[:, :], upto[0:E, 0:E], start=True, stop=True)
            pe.matmul(M1[:, 3 * E:4 * E], ntrep[:, :], before[0:E, 0:E], start=True, stop=True).then_inc(s_tp, 1)
            for q in range(NG):
                route_e(q)
            pe.wait_ge(s_tt, 2)
            for k in range(3):
                ins = pe.matmul(M1[:, P * k:P * k + P], t_rep[:, k, :], ident[:, :], start=True, stop=True)
            ins.then_inc(s_tp, 1)

            def take(u, w, read=None):
                pe.wait_ge(e_r[u], w)
                if read is not None:
                    pe.wait_ge(e_xts, read)
                pe.transpose(xp(u), rows_in[:, u, 0:D], ident[:, :]).then_inc(e_xt, 1)

            def up(u, n, w, read=None):
                pe.wait_ge(e_w[u], w)
                pe.wait_ge(e_xts, n)
                if read is not None:
                    pe.wait_ge(e_ha, read)
                    pe.wait_ge(e_hb, read)
                for b in range(HB):
                    ins = pe.matmul(hp(u, b), w1s[:, u, P * b:P * b + P], xgT[:, u, :], start=True, stop=True)
                ins.then_inc(e_h, 1)

            def down(u, n, e, read=None):
                pe.wait_ge(e_ha, n)
                pe.wait_ge(e_hb, n)
                if read is not None:
                    pe.wait_ge(e_ys, read)
                for b in range(HB):
                    ins = pe.matmul(yp(u), hT[:, u, b, :], e[b], start=(b == 0), stop=(b == HB - 1))
                ins.then_inc(e_y, 1)

            def w2_of(e):
                return [w2s[:, bass.ds(e, 1), b, :].rearrange("p e d -> p (e d)") for b in range(HB)]

            def expert(t):
                return pe.value_load(etab[0:1, 0, t], min_val=0, max_val=E - 1)

            pe.wait_ge(d_w2, 16)
            pe.wait_ge(s_tab, 3)
            pe.wait_ge(s_base, NG)
            for s in range(U):
                take(s, 16, s - 1 if s >= 2 else None)
                if s >= 1:
                    up(s - 1, s, 16, s - 2 if s >= 3 else None)
                if s >= 2:
                    down(s - 2, s - 1, w2_of(expert(slice(s - 2, s - 1))))
            with pe.Fori(1, TILES // U) as i:
                for u in range(U):
                    e = expert(bass.ds(i * U + (u - 2), 1))
                    take(u, i * 16 + 16, i * U + (u - 1))
                    up((u - 1) % U, i * U + u, i * 16 + (16 if u else 0), i * U + (u - 2))
                    down((u - 2) % U, i * U + (u - 1), w2_of(e), i * U + (u - 3))
            up(U - 1, TILES, 16 * (TILES // U), TILES - 2)
            down(U - 2, TILES - 1, w2_of(expert(slice(TILES - 2, TILES - 1))), TILES - 3)
            down(U - 1, TILES, w2_of(expert(slice(TILES - 1, TILES))), TILES - 2)


def kernel(**inputs):
    import numpy as np
    import concourse.bacc as bacc
    from concourse.bass_utils import run_bass_kernel_spmd

    a = {k: np.asarray(v) for k, v in inputs.items()}
    e, d, hid = a["L0_ffn_W1"].shape
    b1 = a["L0_ffn_b1"].reshape(e, hid // 128, 128).transpose(0, 2, 1)
    arrays = {
        "x": a["x"],
        "adj": a["adj"],
        "w": a["L0_gnn_W"],
        "w_t": a["L0_gnn_W"].T,
        "b_w": a["L0_gnn_b_W"],
        "a_vec": a["L0_gnn_a_vec"].reshape(2, d).T,
        "b_a": a["L0_gnn_b_a"],
        "wr": a["L0_ffn_Wr"],
        "br": a["L0_ffn_br"],
        "w1b": np.concatenate([a["L0_ffn_W1"], b1], axis=2),
        "w2": a["L0_ffn_W2"].reshape(e, hid // 128, 128, d).transpose(2, 0, 1, 3),
        "b2": a["L0_ffn_b2"],
    }
    arrays = {k: np.ascontiguousarray(v) for k, v in arrays.items()}
    nc = bacc.Bacc("TRN2", target_bir_lowering=False, num_devices=1)
    aps = [nc.dram_tensor(f"in_{k}", v.shape, mybir.dt.from_np(v.dtype), kind="ExternalInput").ap() for k, v in arrays.items()]
    out = nc.dram_tensor("out", a["x"].shape, mybir.dt.float32, kind="ExternalOutput").ap()
    build(nc, *aps, out)
    r = run_bass_kernel_spmd(nc, [{f"in_{k}": v for k, v in arrays.items()}], core_ids=[0])
    return r.results[0]["out"]
```

```python
from contextlib import ExitStack

import concourse.bass as bass
from concourse import mybir


def build(nc, x, adj, weights, biases, w1b, w2, b2, out):
    F32, BF16, I32, U32 = mybir.dt.float32, mybir.dt.bfloat16, mybir.dt.int32, mybir.dt.uint32
    ALU, ACT = mybir.AluOpType, mybir.ActivationFunctionType
    AX = mybir.AxisListType

    P = 128
    N, D = x.shape
    T = N // P
    E = b2.shape[0]
    HID = w2.shape[2] * P
    HB = HID // P
    TOPK = 2
    GRP = 4
    START = [0, 4, 8, 12, 14, T]
    NG = len(START) - 1
    SIZE = [START[q + 1] - START[q] for q in range(NG)]
    CB = 4
    W1W = HID + HB
    ROW = D + 2
    ID_COL, GATE_COL = D, D + 1
    MAX_TILES = TOPK * N // P + E - 1
    U = 8
    UW = 4
    TILES = -(-MAX_TILES // U) * U
    assert TILES <= P
    EPS = 1e-5
    SLOPE = 0.2
    PENALTY = -(2.0 ** 53)
    SKIP = 1 << 20
    LOWEST = -3.0e38

    ctx = ExitStack()
    with ctx:
        def sb(name, shape, dt=F32):
            return ctx.enter_context(nc.sbuf_tensor(name, shape, dt))

        def sem(name):
            return ctx.enter_context(nc.semaphore(name))

        table = nc.dram_tensor("table", (E * N, ROW), F32, kind="Internal").ap()
        result = nc.dram_tensor("result", (TOPK * N, D), F32, kind="Internal").ap()

        arena = sb("arena", [P, 12 * N + 2 * T])

        def carver(at):
            def carve(width, *dims):
                view = arena[:, at[0]:at[0] + width]
                at[0] += width
                return view
            return carve

        carve = carver([0])
        adj_r = carve(4 * N).bitcast(I32).rearrange("p (s n) -> p s n", s=4)
        z_r = carve(3 * N).rearrange("p (s n) -> p s n", s=3)
        pt_r = carve(2 * T * P).rearrange("p (s t i) -> p s t i", s=2, t=T)
        trow = carve(N)
        h = carve(T * (D + 2)).rearrange("p (t d) -> p t d", t=T)
        pen = carve(N).bitcast(BF16).rearrange("p (s n) -> p s n", s=2)

        carve = carver([0])
        w1a = carve(E * W1W).rearrange("p (e w) -> p e w", e=E)
        rows_in = carve(U * ROW).rearrange("p (u w) -> p u w", u=U)
        xgT = carve(U * P).rearrange("p (u i) -> p u i", u=U)
        hT = carve(U * HB * P).rearrange("p (u b i) -> p u b i", u=U, b=HB)
        ys = carve(U * D).rearrange("p (u d) -> p u d", u=U)
        w1s = carve(UW * W1W).rearrange("p (u w) -> p u w", u=UW)
        t_rep = carve(3 * P).rearrange("p (k i) -> p k i", k=3)
        etab = carve(2 * P).bitcast(I32).rearrange("p (k i) -> p k i", k=2)
        skip = carve(P)
        crow, strow, tg, t_hot = (carve(E) for _ in range(4))
        t_junk = carve(2 * E).rearrange("p (k e) -> p k e", k=2)
        combT = arena[0:E, 2 * N:3 * N]
        zl = arena[:, 0:2 * N].rearrange("p (k t d) -> p k t d", k=TOPK, t=T)
        xh, xhT = z_r[:, 0, :].rearrange("p (t d) -> p t d", t=T), z_r[:, 1, :]

        s8 = sb("s8", [P, T])
        fill = sb("fill", [P, ROW])
        xs = sb("xs", [P, T, D])
        w2s = sb("w2s", [P, E, HB, D])
        store_row = sb("store_row", [P, U], I32)
        rows_out = sb("rows_out", [P, T, TOPK, ROW])
        x2T = sb("x2T", [P, GRP * P])
        a2rep, bwrep, a2w = (x2T[:, k * P:(k + 1) * P] for k in range(3))
        ident = sb("ident", [P, P])
        before = sb("before", [P, P], BF16)
        upto = sb("upto", [P, P], BF16)
        ones = sb("ones", [P, P], BF16)
        iota_e = sb("iota_e", [P, E])
        iota_i = sb("iota_i", [P, E], I32)
        pidx_i = sb("pidx_i", [P, 1], I32)
        pidx = sb("pidx", [P, 1])
        ids = sb("ids", [P, T, TOPK], I32)
        expo = sb("expo", [P, T])
        wts = sb("wts", [P, 2 * D + E + 4])
        w_s, wt_s, wr_s = wts[:, 0:D], wts[:, D:2 * D + 1], wts[:, 2 * D + 1:2 * D + 1 + E]
        a_s, bw_c = wts[:, 2 * D + 1 + E:2 * D + 3 + E], wts[:, 2 * D + 3 + E:2 * D + 4 + E]
        a_sum = sb("a_sum", [P, 1])
        bss = sb("bss", [P, D + 1 + E])
        hbias, br_s = bss[:, 0:D + 1], bss[:, D + 1:D + 1 + E]
        b2_s = sb("b2_s", [E, D])
        st = sb("st", [P, T, 6])
        mv = sb("mv", [P, T, 2])
        ve = sb("ve", [P, T])
        rstd = sb("rstd", [P, T])
        st2 = sb("st2", [P, T, 6])
        mv2 = sb("mv2", [P, T, 2])
        ve2 = sb("ve2", [P, T])
        rstd2 = sb("rstd2", [P, T])
        tmax = sb("tmax", [P, T])
        r8 = sb("r8", [P, T])
        v2 = sb("v2", [P, T])
        c_lo = sb("c_lo", [P, T])
        c_hi = sb("c_hi", [P, T])
        rinv = sb("rinv", [P, T])
        lg = sb("lg", [P, GRP, E])
        top8 = sb("top8", [P, GRP, 8])
        idx8 = sb("idx8", [P, GRP, 8], U32)
        idxf = sb("idxf", [P, GRP, TOPK])
        hot = sb("hot", [P, TOPK, GRP, E])
        both = sb("both", [P, T, E], BF16)
        cnt = sb("cnt", [P, NG + 1, E], BF16)
        cnt_t = sb("cnt_t", [P, 2, E], BF16)
        rk = sb("rk", [P, TOPK, GRP, E])
        rank = sb("rank", [P, TOPK, GRP])
        posf = sb("posf", [P, TOPK, GRP])
        pos = sb("pos", [P, T, TOPK], I32)
        gd = sb("gd", [P, GRP])
        ge = sb("ge", [P, GRP])
        gs = sb("gs", [P, GRP])
        gate = sb("gate", [P, TOPK, GRP])
        cm = rk
        nm2 = sb("nm2", [P, T])
        comb = sb("comb", [P, T, E])
        ci = sb("ci", [E, 1], I32)
        ci2 = sb("ci2", [E, 1], I32)
        ntf = sb("ntf", [E, 1])
        ntrep = sb("ntrep", [E, P], BF16)
        t_e = sb("t_e", [P, 1])
        t_c = sb("t_c", [P, 1])
        t_s = sb("t_s", [P, 1])
        t_k = sb("t_k", [P, 1])
        t_last = sb("t_last", [P, 1])
        t_start = sb("t_start", [P, 1])
        t_ec = sb("t_ec", [P, 1])
        t_vals = sb("t_vals", [P, 3])
        bank = [ctx.enter_context(nc.psum_tensor(f"bank{i}", [P, 512], F32)) for i in range(8)]
        OB, M0, M1 = bank[4:6], bank[6], bank[7]

        d_x = [sem(f"d_x{i}") for i in range(4)]
        d_small = sem("d_small")
        d_w2 = sem("d_w2")
        d_adj = [sem(f"d_adj{i}") for i in range(4)]
        d_fill = sem("d_fill")
        d_put = sem("d_put")
        s_const = sem("s_const")
        s_pool = sem("s_pool")
        s_fill = sem("s_fill")
        s_prep = sem("s_prep")
        s_stat = sem("s_stat")
        s_rstd = sem("s_rstd")
        s_norm = sem("s_norm")
        s_xT = sem("s_xT")
        s_xTs = sem("s_xTs")
        s_wa = sem("s_wa")
        s_was = sem("s_was")
        s_tr = sem("s_tr")
        s_trs = sem("s_trs")
        s_h = sem("s_h")
        s_hs = sem("s_hs")
        s_pen = sem("s_pen")
        s_z = sem("s_z")
        s_s8 = sem("s_s8")
        s_rv = sem("s_rv")
        s_lo = sem("s_lo")
        s_hi = sem("s_hi")
        s_low = sem("s_low")
        s_lk = sem("s_lk")
        s_pt = sem("s_pt")
        s_ea = sem("s_ea")
        s_o = sem("s_o")
        s_ri = sem("s_ri")
        s_x1 = sem("s_x1")
        s_st2 = sem("s_st2")
        s_mv2 = sem("s_mv2")
        s_ve2 = sem("s_ve2")
        s_rstd2 = sem("s_rstd2")
        s_row = sem("s_row")
        s_x2t = sem("s_x2t")
        s_x2s = sem("s_x2s")
        s_lgp = sem("s_lgp")
        s_lg = sem("s_lg")
        s_dve = sem("s_dve")
        s_gd = sem("s_gd")
        s_ge = sem("s_ge")
        s_gate = sem("s_gate")
        s_hot = sem("s_hot")
        s_both = sem("s_both")
        s_cnt = sem("s_cnt")
        s_rk = sem("s_rk")
        s_pos = sem("s_pos")
        s_comb = sem("s_comb")
        s_pl = sem("s_pl")
        s_ct = sem("s_ct")
        s_cts = sem("s_cts")
        s_b2 = sem("s_b2")
        s_base = sem("s_base")
        s_tp = sem("s_tp")
        s_tt = sem("s_tt")
        s_tab = sem("s_tab")
        e_r = [sem(f"e_r{i}") for i in range(U)]
        e_put = [sem(f"e_put{i}") for i in range(U)]
        e_xt = sem("e_xt")
        e_xts = sem("e_xts")
        e_h = sem("e_h")
        e_ha = sem("e_ha")
        e_hb = sem("e_hb")
        e_y = sem("e_y")
        e_ys = sem("e_ys")
        e_id = sem("e_id")
        d_z = [sem(f"d_z{i}") for i in range(4)]
        s_f1 = sem("s_f1")
        s_f2 = sem("s_f2")
        d_out = sem("d_out")

        d_w1 = sem("d_w1")
        s_nm2 = sem("s_nm2")
        s_eng = sem("s_eng")
        e_wc = sem("e_wc")
        block = ctx.enter_context(nc.Block())

        def xp(u):
            return bank[u % 2][:, 0:P]

        def hp(u, b):
            return bank[2 + 2 * b + u % 2][:, 0:P]

        def yp(u):
            return bank[6 + u % 2][:, 0:D]

        def low(t):
            return adj_r[:, t % 4, :].bitcast(F32)

        def numbers(engine, name):
            return [engine.alloc_register(f"{name}{u}") for u in range(U)]

        @block.sync
        def _(sp):
            xt = x.rearrange("(t p) d -> p t d", p=P)
            for c in range(4):
                sp.dma_start(xs[:, 4 * c:4 * c + 4, :], xt[:, 4 * c:4 * c + 4, :]).then_inc(d_x[c], 16)
            FILLS = 8
            padded = table.rearrange("(e n) w -> n e w", e=E)[0:P, :, :]
            for t in range(T):
                if t >= 4:
                    sp.wait_ge(s_lk, t - 3)
                sp.dma_start(adj_r[:, t % 4, :], adj[t * P:(t + 1) * P, :]).then_inc(d_adj[t % 4], 16)
                if 4 <= t < 4 + FILLS:
                    e0, ne = (t - 4) * (E // FILLS), E // FILLS
                    if t == 4:
                        sp.wait_ge(s_fill, 3)
                    sp.dma_start(padded[:, e0:e0 + ne, :],
                                 fill[:, :].rearrange("p (e w) -> p e w", e=1).to_broadcast([P, ne, ROW])).then_inc(d_fill, 16)
                if t >= 12:
                    e0, ne = (t - 12) * (E // 4), E // 4
                    sp.dma_start(w2s[:, e0:e0 + ne, :, :], w2[:, e0:e0 + ne, :, :]).then_inc(d_w2, 16)

            CH = 8
            for c in range(E // CH):
                last = (c + 1) * CH * W1W
                if last <= 4 * N:
                    sp.wait_ge(s_lk, T)
                elif last <= 7 * N:
                    sp.wait_ge(s_pt, 4 * T)
                else:
                    sp.wait_ge(s_o, T)
                sp.dma_start(w1a[:, c * CH:(c + 1) * CH, :], w1b[:, c * CH:(c + 1) * CH, :]).then_inc(d_w1, 16)

            sp.wait_ge(s_tab, 3)
            first_row = numbers(sp, "first_row")
            sp.wait_ge(d_put, 16 * TOPK * T)
            sp.load(first_row, etab[0:1, 1, 0:U])
            for u in range(U):
                r = sp.snap(first_row[u], min_val=0, max_val=E * N - P)
                sp.dma_start(rows_in[:, u, :], table[bass.ds(r, P), :]).then_inc(e_r[u], 16)
            with sp.Fori(1, TILES // U) as i:
                sp.load(first_row, etab[0:1, 1, bass.ds(i * U, U)])
                for u in range(U):
                    r = sp.snap(first_row[u], min_val=0, max_val=E * N - P)
                    sp.wait_ge(e_ys, i * U + (u + 1 - U))
                    sp.wait_ge(e_id, i * U + (u + 1 - U))
                    sp.dma_start(rows_in[:, u, :], table[bass.ds(r, P), :]).then_inc(e_r[u], 16)

            for u in range(U):
                sp.wait_ge(e_put[u], 16 * (TILES // U))
            zt = result.rearrange("(k t p) d -> p k t d", k=TOPK, p=P)
            for c in range(4):
                for k in range(TOPK):
                    sp.dma_start(zl[:, k, 4 * c:4 * c + 4, :], zt[:, k, 4 * c:4 * c + 4, :]).then_inc(d_z[c], 16)
            ot = out.rearrange("(t p) d -> p t d", p=P)
            for c in range(4):
                sp.wait_ge(s_f2, c + 1)
                sp.dma_start(ot[:, 4 * c:4 * c + 4, :], xs[:, 4 * c:4 * c + 4, :]).then_inc(d_out, 16)
            sp.wait_ge(d_out, 64)

        @block.gpsimd
        def _(pool):
            def link(ins, n=[0]):
                n[0] += 1
                ins.then_inc(s_pl, 1)
                pool.wait_ge(s_pl, n[0])

            pool.memset(expo[:, :], -0.5)
            link(pool.memset(ident[:, :], 0.0))
            pool.affine_select(out=ident[:, :], in_=ident[:, :], compare_op=ALU.not_equal, fill=1.0,
                               base=0, pattern=[[-1, P]], channel_multiplier=1).then_inc(s_const, 1)
            pool.memset(fill[:, :], 0.0).then_inc(s_fill, 1)
            pool.wait_ge(s_fill, 1)
            pool.memset(fill[:, ID_COL:ID_COL + 1].bitcast(I32), SKIP).then_inc(s_fill, 2)
            pool.memset(h[:, :, D + 1:D + 2], 1.0).then_inc(s_pool, 1)
            link(pool.memset(ones[:, :], 1.0))
            pool.affine_select(out=before[:, :], in_=ones[:, :], compare_op=ALU.is_gt, fill=0.0,
                               base=0, pattern=[[1, P]], channel_multiplier=-1).then_inc(s_pool, 1)
            pool.affine_select(out=upto[:, :], in_=ones[:, :], compare_op=ALU.is_ge, fill=0.0,
                               base=0, pattern=[[1, P]], channel_multiplier=-1).then_inc(s_pool, 1)
            pool.iota(iota_i[:, :], pattern=[[1, E]], base=0, channel_multiplier=0)
            pool.iota(ids[:, :, :], pattern=[[P, T], [N, TOPK]], base=0, channel_multiplier=1)
            link(pool.iota(pidx_i[:, :], pattern=[[1, 1]], base=0, channel_multiplier=1))
            pool.tensor_copy(iota_e[:, :], iota_i[:, :])
            pool.tensor_copy(pidx[:, :], pidx_i[:, :])
            pool.memset(cnt[:, 0, :], 0.0).then_inc(s_pool, 1)
            pool.wait_ge(s_stat, 1)
            pool.tensor_tensor(rstd[:, :], ve[:, :], expo[:, :], ALU.pow).then_inc(s_rstd, 1)

            def rstd_of(t):
                pool.wait_ge(s_mv2, t + 1)
                pool.tensor_scalar(ve2[:, t:t + 1], mv2[:, t, 1:2], EPS, None, ALU.add).then_inc(s_ve2, 1)
                pool.wait_ge(s_ve2, t + 1)
                pool.tensor_tensor(rstd2[:, t:t + 1], ve2[:, t:t + 1], expo[:, 0:1], ALU.pow).then_inc(s_rstd2, 1)
                pool.wait_ge(s_rstd2, t + 1)
                pool.tensor_scalar(nm2[:, t:t + 1], mv2[:, t, 0:1], rstd2[:, t:t + 1], -1.0, ALU.mult, ALU.mult).then_inc(s_nm2, 1)

            def counts(q):
                pool.wait_ge(s_both, q + 1)
                b = both[:, START[q]:START[q + 1], :]
                n = SIZE[q] // 2
                last = pool.tensor_tensor(cnt_t[:, 0:n, :], b[:, 0:n, :], b[:, n:2 * n, :], ALU.add)
                if n == 2:
                    link(last)
                    last = pool.tensor_tensor(cnt_t[:, 0, :], cnt_t[:, 0, :], cnt_t[:, 1, :], ALU.add)
                link(last)
                pool.tensor_tensor(cnt[:, q + 1, :], cnt[:, q, :], cnt_t[:, 0, :], ALU.add).then_inc(s_cnt, 1)

            def place(q, t):
                pool.wait_ge(s_pos, q + 1)
                for k in range(TOPK):
                    pool.indirect_dma_start(table[:, :], bass.IndirectOffsetOnAxis(pos[:, t, k:k + 1], 0),
                                            rows_out[:, t, k, :], None).then_inc(d_put, 16)

            def combine(q):
                n = SIZE[q]
                for k in range(TOPK):
                    ins = pool.tensor_tensor(cm[:, k, 0:n, :], hot[:, k, 0:n, :],
                                             gate[:, k, 0:n].rearrange("p (g e) -> p g e", e=1).to_broadcast([P, n, E]), ALU.mult)
                link(ins)
                pool.tensor_tensor(comb[:, START[q]:START[q + 1], :], cm[:, 0, 0:n, :], cm[:, 1, 0:n, :], ALU.add).then_inc(s_comb, 1)

            for s in range(3, T + 12):
                if 0 <= s - 3 < T:
                    rstd_of(s - 3)
                if s == START[1] + 9:
                    pool.wait_ge(d_fill, 16 * 8)
                for q in range(NG):
                    z = START[q + 1]
                    if s == z + 7:
                        counts(q)
                    if s == z + 9:
                        place(q, START[q])
                        if q < NG - 1:
                            combine(q)
                    if z + 9 < s < z + 9 + SIZE[q]:
                        place(q, START[q] + s - (z + 9))
            combine(NG - 1)

            limit = pool.alloc_register("last_result_row")
            pool.reg_mov(limit, TOPK * N - 1)
            for u in range(U):
                pool.wait_ge(e_ys, u + 1)
                pool.wait_ge(e_id, u + 1)
                pool.indirect_dma_start(result[:, :], bass.IndirectOffsetOnAxis(store_row[:, u:u + 1], 0),
                                        ys[:, u, :], None, bounds_check=limit, oob_is_err=False).then_inc(e_put[u], 16)
            tile = pool.alloc_register("tiles_stored")
            pool.reg_mov(tile, U + 1)
            with pool.Fori(1, TILES // U) as i:
                for u in range(U):
                    pool.wait_ge(e_ys, tile)
                    pool.wait_ge(e_id, tile)
                    pool.reg_add(tile, tile, 1)
                    pool.indirect_dma_start(result[:, :], bass.IndirectOffsetOnAxis(store_row[:, u:u + 1], 0),
                                            ys[:, u, :], None, bounds_check=limit, oob_is_err=False).then_inc(e_put[u], 16)

        @block.scalar
        def _(act):
            act.dma_start(wts[:, :], weights).then_inc(d_small, 16)
            act.dma_start(bss[:, :], biases.to_broadcast([P, D + 1 + E])).then_inc(d_small, 16)
            act.dma_start(b2_s[:, :], b2).then_inc(d_small, 16)
            for b in range(4):
                act.wait_ge(s_xT, b + 1)
                act.activation(xhT[:, 512 * b:512 * b + 512], bank[b][:, :], ACT.Copy).then_inc(s_xTs, 1)
            for b in range(4):
                act.wait_ge(s_tr, b + 1)
                act.activation(trow[:, 512 * b:512 * b + 512], bank[b][:, :], ACT.Copy).then_inc(s_trs, 1)

            def scores(t):
                if t == 0:
                    act.wait_ge(s_s8, 1)
                act.wait_ge(s_z, t + 1)
                act.activation(r8[:, t:t + 1], tmax[:, t:t + 1], ACT.Relu, bias=s8[:, t:t + 1], scale=1.0 - SLOPE).then_inc(s_rv, 1)
                act.activation(v2[:, t:t + 1], tmax[:, t:t + 1], ACT.Copy, scale=-SLOPE).then_inc(s_rv, 1)
                act.wait_ge(s_rv, 2 * (t + 1))
                act.activation(c_lo[:, t:t + 1], r8[:, t:t + 1], ACT.Identity, bias=v2[:, t:t + 1], scale=-1.0).then_inc(s_lo, 1)
                act.wait_ge(s_lo, t + 1)
                act.activation(low(t), z_r[:, t % 3, :], ACT.Identity, bias=c_lo[:, t:t + 1], scale=SLOPE).then_inc(s_low, 1)
                act.activation(c_hi[:, t:t + 1], c_lo[:, t:t + 1], ACT.Identity, bias=s8[:, t:t + 1]).then_inc(s_hi, 1)

            def evac(t):
                for b in range(4):
                    act.wait_ge(s_pt, 4 * t + b + 1)
                    if t >= 2:
                        act.wait_ge(s_o, t - 1)
                    act.activation(pt_r[:, t % 2, CB * b:CB * b + CB, :].rearrange("p c i -> p (c i)"),
                                   bank[b][:, :], ACT.Exp).then_inc(s_ea, 1)

            def norm(t):
                act.wait_ge(s_nm2, t + 1)
                act.activation(rows_out[:, t, :, 0:D],
                               xs[:, t, :].rearrange("p (k d) -> p k d", k=1).to_broadcast([P, TOPK, D]),
                               ACT.Identity, bias=nm2[:, t:t + 1], scale=rstd2[:, t:t + 1]).then_inc(s_row, 1)

            def route_a(q):
                act.wait_ge(s_x2t, q + 1)
                n = SIZE[q] * P
                act.activation(x2T[:, 0:n], M0[:, 0:n], ACT.Copy).then_inc(s_x2s, 1)

            def route_b(q):
                n = SIZE[q]
                act.wait_ge(s_gd, q + 1)
                act.activation(ge[:, 0:n], gd[:, 0:n], ACT.Exp).then_inc(s_ge, 1)

            for s in range(T + 12):
                if s < T:
                    scores(s)
                if 1 <= s <= T:
                    evac(s - 1)
                if 0 <= s - 4 < T:
                    norm(s - 4)
                for q in range(NG):
                    if s == START[q + 1] + 5:
                        route_a(q)
                    if s == START[q + 1] + 8:
                        route_b(q)

            def relu(u, n):
                act.wait_ge(e_h, n)
                act.activation(hT[:, u, 0, :], hp(u, 0), ACT.Relu, bias=w1s[:, u % UW, HID:HID + 1]).then_inc(e_ha, 1)

            def weigh(u, n, stored=None):
                act.wait_ge(e_y, n)
                if stored is not None:
                    act.wait_ge(e_put[u], stored)
                act.activation(ys[:, u, :], yp(u), ACT.Copy, scale=rows_in[:, u, GATE_COL:GATE_COL + 1]).then_inc(e_ys, 1)

            relu(0, 1)
            for u in range(U):
                relu((u + 1) % U, u + 2)
                weigh(u, u + 1)
            with act.Fori(1, TILES // U - 1) as i:
                for u in range(U):
                    relu((u + 1) % U, i * U + (u + 2))
                    weigh(u, i * U + (u + 1), i * 16)
            for u in range(U):
                if u < U - 1:
                    relu(u + 1, TILES - U + u + 2)
                weigh(u, TILES - U + u + 1, 16 * (TILES // U - 1))

            for q in range(NG):
                act.wait_ge(s_ct, q + 1)
                act.activation(combT[:, START[q] * P:START[q + 1] * P], bank[q][0:E, 0:SIZE[q] * P], ACT.Copy).then_inc(s_cts, 1)

        @block.vector
        def _(dve):
            chain = [0]

            def link(ins):
                chain[0] += 1
                ins.then_inc(s_dve, 1)
                dve.wait_ge(s_dve, chain[0])

            dve.wait_ge(d_small, 16 * 3)
            dve.tensor_copy(a2rep[:, :], a_s[:, 1:2].to_broadcast([P, P]))
            dve.tensor_copy(bwrep[:, :], bw_c[:, 0:1].to_broadcast([P, P]))
            dve.tensor_tensor(a_sum[:, :], a_s[:, 0:1], a_s[:, 1:2], ALU.add).then_inc(s_prep, 1)
            for t in range(T):
                if t % 4 == 0:
                    dve.wait_ge(d_x[t // 4], 16)
                ins = dve.bn_stats(st[:, t, :], xs[:, t, :])
            link(ins)
            for t in range(T):
                ins = dve.bn_aggr(mv[:, t, :], st[:, t, :])
            link(ins)
            dve.tensor_scalar(ve[:, :], mv[:, :, 1], EPS, None, ALU.add).then_inc(s_stat, 1)
            dve.wait_ge(s_wa, 1)
            dve.tensor_copy(a2w[:, :], bank[4][:, 0:P])
            dve.tensor_copy(wt_s[:, D:D + 1], bank[5][:, 0:1])
            dve.tensor_tensor(hbias[:, D:D + 1], bank[6][:, 0:1], hbias[:, D:D + 1], ALU.add).then_inc(s_was, 1)
            dve.wait_ge(s_rstd, 1)
            for t in range(T):
                ins = dve.tensor_scalar(xh[:, t, :], xs[:, t, :], mv[:, t, 0:1], rstd[:, t:t + 1], ALU.subtract, ALU.mult)
                if t % 4 == 3:
                    ins.then_inc(s_norm, 1)

            def h_evac(c):
                dve.wait_ge(s_h, c + 1)
                dve.tensor_tensor(h[:, 2 * c:2 * c + 2, 0:D + 1],
                                  bank[(c + 4) % 8][:, 0:2 * (D + 1)].rearrange("p (t d) -> p t d", t=2),
                                  hbias[:, :].rearrange("p (t d) -> p t d", t=1).to_broadcast([P, 2, D + 1]),
                                  ALU.add).then_inc(s_hs, 1)

            def penalty(t):
                dve.wait_ge(d_adj[t % 4], 16 * (t // 4 + 1))
                if t >= 2:
                    dve.wait_ge(s_z, t - 1)
                dve.tensor_scalar(pen[:, t % 2, :], adj_r[:, t % 4, :], 0, PENALTY, ALU.is_le, ALU.mult).then_inc(s_pen, 1)

            def scores(t):
                if t == 0:
                    dve.wait_ge(s_trs, 4)
                    dve.wait_ge(s_h, 8)
                if t >= 3:
                    dve.wait_ge(s_pt, 4 * (t - 2))
                dve.wait_ge(s_pen, t + 1)
                dve.tensor_tensor_reduce(out=z_r[:, t % 3, :], in0=pen[:, t % 2, :], in1=trow[:, :], scale=1.0,
                                         scalar=LOWEST, op0=ALU.add, op1=ALU.max, accum_out=tmax[:, t:t + 1]).then_inc(s_z, 1)

            def leaky(t):
                dve.wait_ge(s_low, t + 1)
                dve.wait_ge(s_hi, t + 1)
                z = z_r[:, t % 3, :]
                dve.scalar_tensor_tensor(z, z, c_hi[:, t:t + 1], low(t), ALU.add, ALU.max).then_inc(s_lk, 1)

            def residual(t):
                dve.wait_ge(s_o, t + 1)
                dve.reciprocal(rinv[:, t:t + 1], OB[t % 2][:, D + 1:D + 2]).then_inc(s_ri, 1)
                dve.wait_ge(s_ri, t + 1)
                dve.scalar_tensor_tensor(xs[:, t, :], OB[t % 2][:, 0:D], rinv[:, t:t + 1], xs[:, t, :],
                                         ALU.mult, ALU.add).then_inc(s_x1, 1)
                dve.wait_ge(s_x1, t + 1)
                dve.bn_stats(st2[:, t, :], xs[:, t, :]).then_inc(s_st2, 1)
                dve.wait_ge(s_st2, t + 1)
                dve.bn_aggr(mv2[:, t, :], st2[:, t, :]).then_inc(s_mv2, 1)

            def top2(q):
                n = SIZE[q]
                dve.wait_ge(s_lgp, q + 1)
                link(dve.tensor_tensor(lg[:, 0:n, :], M1[:, 0:n * E].rearrange("p (g e) -> p g e", g=n),
                                       br_s[:, :].rearrange("p (g e) -> p g e", g=1).to_broadcast([P, n, E]), ALU.add))
                for g in range(n):
                    ins = dve.max(top8[:, g, :], lg[:, g, :])
                link(ins)
                dve.tensor_tensor(gd[:, 0:n], top8[:, 0:n, 1], top8[:, 0:n, 0], ALU.subtract).then_inc(s_gd, 1)
                for g in range(n):
                    ins = dve.max_index(idx8[:, g, :], top8[:, g, :], lg[:, g, :])
                link(ins)
                link(dve.tensor_copy(idxf[:, 0:n, :], idx8[:, 0:n, 0:TOPK]))
                if q >= 1:
                    dve.wait_ge(s_comb, q)
                for k in range(TOPK):
                    ins = dve.tensor_tensor(hot[:, k, 0:n, :],
                                            iota_e[:, :].rearrange("p (g e) -> p g e", g=1).to_broadcast([P, n, E]),
                                            idxf[:, 0:n, k:k + 1].to_broadcast([P, n, E]), ALU.is_equal)
                link(ins)
                dve.tensor_tensor(both[:, START[q]:START[q + 1], :], hot[:, 0, 0:n, :], hot[:, 1, 0:n, :], ALU.add).then_inc(s_both, 1)

            def place(q):
                n = SIZE[q]
                rows = slice(START[q], START[q + 1])
                dve.wait_ge(s_ge, q + 1)
                link(dve.tensor_scalar(gs[:, 0:n], ge[:, 0:n], 1.0, None, ALU.add))
                link(dve.reciprocal(gate[:, 0, 0:n], gs[:, 0:n]))
                dve.tensor_tensor(gate[:, 1, 0:n], ge[:, 0:n], gate[:, 0, 0:n], ALU.mult).then_inc(s_gate, 1)
                dve.wait_ge(s_rk, q + 1)
                for k in range(TOPK):
                    ins = dve.tensor_tensor(rk[:, k, 0:n, :], M1[:, 256:256 + n * E].rearrange("p (g e) -> p g e", g=n),
                                            hot[:, k, 0:n, :], ALU.mult)
                link(ins)
                link(dve.tensor_reduce(rank[:, :, 0:n], rk[:, :, 0:n, :], AX.X, ALU.add))
                link(dve.scalar_tensor_tensor(posf[:, :, 0:n], idxf[:, 0:n, :].rearrange("p g k -> p k g"), float(N),
                                              rank[:, :, 0:n], ALU.mult, ALU.add))
                dve.wait_ge(s_gate, q + 1)
                dve.tensor_copy(rows_out[:, rows, :, ID_COL].bitcast(I32), ids[:, rows, :])
                dve.tensor_copy(rows_out[:, rows, :, GATE_COL], gate[:, :, 0:n].rearrange("p k g -> p g k"))
                dve.tensor_copy(pos[:, rows, :].rearrange("p g k -> p k g"), posf[:, :, 0:n]).then_inc(s_pos, 1)

            def base(q):
                dve.wait_ge(s_b2, q + 1)
                xq = xs[:, START[q]:START[q + 1], :].rearrange("p g d -> p (g d)")
                dve.tensor_tensor(xq, xq, bank[q][:, 0:SIZE[q] * P], ALU.add).then_inc(s_base, 1)

            penalty(0)
            for c in range(8):
                h_evac(c)
            dve.wait_ge(s_hs, 8)
            dve.tensor_scalar(s8[:, :], h[:, :, D], 1.0 - SLOPE, None, ALU.mult).then_inc(s_s8, 1)
            dve.wait_ge(s_pool, 4)
            for s in range(T + 12):
                if s < T:
                    scores(s)
                if s + 1 < T:
                    penalty(s + 1)
                if 1 <= s <= T:
                    leaky(s - 1)
                if 0 <= s - 3 < T:
                    residual(s - 3)
                for q in range(NG):
                    if s == START[q + 1] + 7:
                        top2(q)
                    if s == START[q + 1] + 9:
                        place(q)

            dve.wait_ge(s_tp, 1)
            link(dve.tensor_scalar(ci[:, :], M1[0:E, 0:1], float(P - 1), None, ALU.add))
            dve.tensor_copy(crow[:, :], M1[:, E:2 * E])
            link(dve.tensor_scalar(ci2[:, :], ci[:, :], P.bit_length() - 1, None, ALU.arith_shift_right))
            link(dve.tensor_copy(ntf[:, :], ci2[:, :]))
            dve.tensor_copy(ntrep[:, :], ntf[:, :].to_broadcast([E, P])).then_inc(s_tt, 1)
            dve.wait_ge(s_tp, 2)
            link(dve.tensor_copy(strow[:, :], M1[:, 3 * E:4 * E]))
            link(dve.tensor_scalar(tg[:, :], M1[:, 2 * E:3 * E], pidx[:, :], None, ALU.is_le))
            link(dve.tensor_reduce(t_e[:, :], tg[:, :], AX.X, ALU.add))
            link(dve.tensor_scalar(t_hot[:, :], iota_e[:, :], t_e[:, :], None, ALU.is_equal))
            dve.tensor_tensor(t_junk[:, 0, :], t_hot[:, :], crow[:, :], ALU.mult)
            link(dve.tensor_tensor(t_junk[:, 1, :], t_hot[:, :], strow[:, :], ALU.mult))
            dve.tensor_reduce(t_c[:, :], t_junk[:, 0, :], AX.X, ALU.add)
            link(dve.tensor_reduce(t_s[:, :], t_junk[:, 1, :], AX.X, ALU.add))
            dve.tensor_scalar(t_last[:, :], t_c[:, :], float(-P), 0.0, ALU.add, ALU.max)
            link(dve.tensor_tensor(t_k[:, :], pidx[:, :], t_s[:, :], ALU.subtract))
            link(dve.tensor_scalar(t_k[:, :], t_k[:, :], float(P), None, ALU.mult))
            dve.tensor_scalar(t_ec[:, :], t_e[:, :], float(E - 1), None, ALU.min)
            link(dve.tensor_tensor(t_start[:, :], t_k[:, :], t_last[:, :], ALU.min))
            dve.tensor_copy(t_vals[:, 0:1], t_ec[:, :])
            dve.scalar_tensor_tensor(t_vals[:, 1:2], t_ec[:, :], float(N), t_start[:, :], ALU.mult, ALU.add)
            link(dve.tensor_tensor(t_vals[:, 2:3], t_k[:, :], t_start[:, :], ALU.subtract))
            dve.tensor_copy(t_rep[:, :, :], t_vals[:, :].rearrange("p (k o) -> p k o", o=1).to_broadcast([P, 3, P])).then_inc(s_tt, 1)
            dve.wait_ge(s_tp, 3)
            dve.tensor_copy(etab[:, :, :], M1[:, 0:2 * P].rearrange("p (k o) -> p k o", k=2)).then_inc(s_tab, 1)
            dve.tensor_scalar(skip[:, :], M1[:, 2 * P:3 * P], pidx[:, :], float(SKIP), ALU.is_gt, ALU.mult).then_inc(s_tab, 2)

            def take(u, n, t, e, stored=None):
                dve.wait_ge(e_xt, n)
                dve.tensor_copy(xgT[:, u, :], xp(u)).then_inc(e_xts, 1)
                e = dve.snap(e, min_val=0, max_val=E - 1)
                dve.tensor_copy(w1s[:, u % UW, :], w1a[:, bass.ds(e, 1), :].rearrange("p e w -> p (e w)")).then_inc(e_wc, 1)
                if stored is not None:
                    dve.wait_ge(e_put[u], stored)
                dve.tensor_tensor(store_row[:, u:u + 1], rows_in[:, u, ID_COL:ID_COL + 1].bitcast(I32), skip[:, t],
                                  ALU.add).then_inc(e_id, 1)

            def relu(u, n):
                dve.wait_ge(e_h, n)
                dve.tensor_scalar(hT[:, u, 1, :], hp(u, 1), w1s[:, u % UW, HID + 1:HID + 2], 0.0, ALU.add, ALU.max).then_inc(e_hb, 1)

            dve.wait_ge(s_tab, 3)
            dve.wait_ge(d_w1, 16 * (E // 8))
            expert = numbers(dve, "expert")
            dve.load(expert, etab[0:1, 0, 0:U])
            for u in range(U):
                take(u, u + 1, slice(u, u + 1), expert[u])
                if u:
                    relu(u - 1, u)
            with dve.Fori(1, TILES // U) as i:
                dve.load(expert, etab[0:1, 0, bass.ds(i * U, U)])
                for u in range(U):
                    take(u, i * U + (u + 1), bass.ds(i * U + u, 1), expert[u], i * 16)
                    relu((u - 1) % U, i * U + u)
            relu(U - 1, TILES)

            for q in range(NG):
                base(q)
            for c in range(4):
                dve.wait_ge(d_z[c], 32)
                if c == 0:
                    dve.wait_ge(s_base, NG)
                xc = xs[:, 4 * c:4 * c + 4, :]
                dve.tensor_tensor(xc, xc, zl[:, 0, 4 * c:4 * c + 4, :], ALU.add).then_inc(s_f1, 1)
                dve.wait_ge(s_f1, c + 1)
                dve.tensor_tensor(xc, xc, zl[:, 1, 4 * c:4 * c + 4, :], ALU.add).then_inc(s_f2, 1)

        @block.tensor
        def _(pe):
            pe.wait_ge(s_prep, 1)
            pe.matmul(bank[4][:, 0:P], w_s[:, :], a2rep[:, :], start=True, stop=True)
            pe.matmul(bank[5][:, 0:1], w_s[:, :], a_s[:, 0:1], start=True, stop=True)
            pe.matmul(bank[6][:, 0:1], bwrep[:, :], a_sum[:, :], start=True, stop=True).then_inc(s_wa, 1)
            pe.wait_ge(s_const, 1)
            for b in range(4):
                pe.wait_ge(s_norm, b + 1)
                for c in range(CB):
                    ins = pe.transpose(bank[b][:, P * c:P * c + P], xh[:, CB * b + c, :], ident[:, :])
                ins.then_inc(s_xT, 1)
            pe.wait_ge(s_was, 1)
            for b in range(4):
                pe.wait_ge(s_xTs, b + 1)
                pe.matmul(bank[b][:, :], a2w[:, :], xhT[:, 512 * b:512 * b + 512], start=True, stop=True).then_inc(s_tr, 1)
            for c in range(8):
                if c >= 4:
                    pe.wait_ge(s_trs, c - 3)
                for j in range(2):
                    t = 2 * c + j
                    ins = pe.matmul(bank[(c + 4) % 8][:, j * (D + 1):(j + 1) * (D + 1)], xhT[:, P * t:P * t + P],
                                    wt_s[:, :], start=True, stop=True)
                ins.then_inc(s_h, 1)

            def turn(t):
                pe.wait_ge(s_lk, t + 1)
                for b in range(4):
                    if t == 0:
                        pe.wait_ge(s_hs, 8)
                    else:
                        pe.wait_ge(s_ea, 4 * (t - 1) + b + 1)
                    for c in range(CB):
                        j = CB * b + c
                        ins = pe.transpose(bank[b][:, P * c:P * c + P], z_r[:, t % 3, P * j:P * j + P], ident[:, :])
                    ins.then_inc(s_pt, 1)

            def attend(t):
                if t >= 2:
                    pe.wait_ge(s_x1, t - 1)
                for j in range(T):
                    b = j // CB
                    if j % CB == 0:
                        pe.wait_ge(s_ea, 4 * t + b + 1)
                    ins = pe.matmul(OB[t % 2][:, 0:D + 2], pt_r[:, t % 2, j, :], h[:, j, :], start=(j == 0), stop=(j == T - 1))
                ins.then_inc(s_o, 1)

            def route_a(q):
                pe.wait_ge(s_row, START[q + 1])
                if q >= 1:
                    pe.wait_ge(s_x2s, q)
                for g in range(SIZE[q]):
                    ins = pe.transpose(M0[:, P * g:P * g + P], rows_out[:, START[q] + g, 0, 0:D], ident[:, :])
                ins.then_inc(s_x2t, 1)

            def route_b(q):
                pe.wait_ge(s_x2s, q + 1)
                if q >= 1:
                    pe.wait_ge(s_pos, q)
                for g in range(SIZE[q]):
                    ins = pe.matmul(M1[:, E * g:E * g + E], x2T[:, P * g:P * g + P], wr_s[:, :], start=True, stop=True)
                ins.then_inc(s_lgp, 1)

            def route_c(q):
                pe.wait_ge(s_both, q + 1)
                if q >= 1:
                    pe.wait_ge(s_cnt, q)
                for g in range(SIZE[q]):
                    rows = [(before, both[:, START[q] + g, :]), (ones, cnt[:, q, :])]
                    rows += [(ones, both[:, START[q] + j, :]) for j in range(g)]
                    for n, (lt, r) in enumerate(rows):
                        ins = pe.matmul(M1[:, 256 + E * g:256 + E * g + E], lt[:, :], r, start=(n == 0), stop=(n == len(rows) - 1))
                ins.then_inc(s_rk, 1)

            for s in range(T + 12):
                if s < T:
                    turn(s)
                if 1 <= s <= T:
                    attend(s - 1)
                for q in range(NG):
                    if s == START[q + 1] + 4:
                        route_a(q)
                    if s == START[q + 1] + 5:
                        route_b(q)
                    if s == START[q + 1] + 7:
                        route_c(q)

            pe.wait_ge(s_cnt, NG)
            pe.wait_ge(s_pos, NG)
            total = cnt[:, NG, :]
            pe.matmul(M1[0:E, 0:1], total, ones[:, 0:1], start=True, stop=True)
            pe.matmul(M1[:, E:2 * E], ones[:, :], total, start=True, stop=True).then_inc(s_tp, 1)
            pe.wait_ge(s_tt, 1)
            pe.matmul(M1[:, 2 * E:3 * E], ntrep[:, :], upto[0:E, 0:E], start=True, stop=True)
            pe.matmul(M1[:, 3 * E:4 * E], ntrep[:, :], before[0:E, 0:E], start=True, stop=True).then_inc(s_tp, 1)
            pe.wait_ge(s_tt, 2)
            for k in range(3):
                ins = pe.matmul(M1[:, P * k:P * k + P], t_rep[:, k, :], ident[:, :], start=True, stop=True)
            ins.then_inc(s_tp, 1)

            def take(u, w):
                pe.wait_ge(e_r[u], w)
                pe.transpose(xp(u), rows_in[:, u, 0:D], ident[:, :]).then_inc(e_xt, 1)

            def up(u, n):
                pe.wait_ge(e_wc, n)
                for b in range(HB):
                    ins = pe.matmul(hp(u, b), w1s[:, u % UW, P * b:P * b + P], xgT[:, u, :], start=True, stop=True)
                ins.then_inc(e_h, 1)

            def down(u, n, e):
                e = pe.snap(e, min_val=0, max_val=E - 1)
                pe.wait_ge(e_ha, n)
                pe.wait_ge(e_hb, n)
                for b in range(HB):
                    ins = pe.matmul(yp(u), hT[:, u, b, :], w2s[:, bass.ds(e, 1), b, :].rearrange("p e d -> p (e d)"),
                                    start=(b == 0), stop=(b == HB - 1))
                ins.then_inc(e_y, 1)

            pe.wait_ge(d_w2, 16 * 4)
            pe.wait_ge(s_tab, 3)
            expert = numbers(pe, "expert")
            take(0, 16)
            take(1, 16)
            up(0, 1)
            with pe.Fori(0, TILES // U - 1) as i:
                pe.load(expert, etab[0:1, 0, bass.ds(i * U, U)])
                for u in range(U):
                    take((u + 2) % U, i * 16 + (16 if u + 2 < U else 32))
                    up((u + 1) % U, i * U + (u + 2))
                    down(u, i * U + (u + 1), expert[u])
            pe.load(expert, etab[0:1, 0, TILES - U:TILES])
            for u in range(U):
                if u + 2 < U:
                    take(u + 2, 16 * (TILES // U))
                if u + 1 < U:
                    up(u + 1, TILES - U + u + 2)
                down(u, TILES - U + u + 1, expert[u])

            pe.wait_ge(e_ys, TILES)
            for q in range(NG):
                pe.wait_ge(s_comb, q + 1)
                for g in range(SIZE[q]):
                    ins = pe.transpose(bank[q][0:E, P * g:P * g + P], comb[:, START[q] + g, :], ident[:, :])
                ins.then_inc(s_ct, 1)
            for q in range(NG):
                pe.wait_ge(s_cts, q + 1)
                for g in range(SIZE[q]):
                    t = START[q] + g
                    ins = pe.matmul(bank[q][:, P * g:P * g + P], combT[:, P * t:P * t + P], b2_s[:, :], start=True, stop=True)
                ins.then_inc(s_b2, 1)


def kernel(**inputs):
    import numpy as np
    import concourse.bacc as bacc
    from concourse.bass_utils import run_bass_kernel_spmd

    a = {k: np.asarray(v) for k, v in inputs.items()}
    e, d, hid = a["L0_ffn_W1"].shape
    b1 = a["L0_ffn_b1"].reshape(e, hid // 128, 128).transpose(0, 2, 1)
    w, av = a["L0_gnn_W"], a["L0_gnn_a_vec"].reshape(2, d)
    arrays = {
        "x": a["x"],
        "adj": a["adj"],
        "weights": np.concatenate([w, w.T, np.zeros((d, 1), w.dtype), a["L0_ffn_Wr"], av.T, a["L0_gnn_b_W"][:, None]], axis=1),
        "biases": np.concatenate([a["L0_gnn_b_W"], a["L0_gnn_b_a"], a["L0_ffn_br"]])[None, :],
        "w1b": np.concatenate([a["L0_ffn_W1"], b1], axis=2).transpose(1, 0, 2),
        "w2": a["L0_ffn_W2"].reshape(e, hid // 128, 128, d).transpose(2, 0, 1, 3),
        "b2": a["L0_ffn_b2"],
    }
    arrays = {k: np.ascontiguousarray(v) for k, v in arrays.items()}
    nc = bacc.Bacc("TRN2", target_bir_lowering=False, num_devices=1)
    aps = [nc.dram_tensor(f"in_{k}", v.shape, mybir.dt.from_np(v.dtype), kind="ExternalInput").ap() for k, v in arrays.items()]
    out = nc.dram_tensor("out", a["x"].shape, mybir.dt.float32, kind="ExternalOutput").ap()
    build(nc, *aps, out)
    r = run_bass_kernel_spmd(nc, [{f"in_{k}": v for k, v in arrays.items()}], core_ids=[0])
    return r.results[0]["out"]
```

```python
from contextlib import ExitStack

import concourse.bass as bass
from concourse import mybir


def build(nc, x, adj, weights, biases, w1b, w2, b2, out):
    F32, BF16, I32, U32 = mybir.dt.float32, mybir.dt.bfloat16, mybir.dt.int32, mybir.dt.uint32
    ALU, ACT = mybir.AluOpType, mybir.ActivationFunctionType
    AX = mybir.AxisListType

    P = 128
    N, D = x.shape
    T = N // P
    E = b2.shape[0]
    HID = w2.shape[2] * P
    HB = HID // P
    TOPK = 2
    GRP = 4
    START = [0, 4, 8, 11, 14, T]
    NG = len(START) - 1
    SIZE = [START[q + 1] - START[q] for q in range(NG)]
    SLOT = [0, GRP, 0, 3, 6]
    COUNTED = 3
    CB = 4
    W1W = HID + HB
    ROW = D + 2
    ID_COL, GATE_COL = D, D + 1
    MAX_TILES = TOPK * N // P + E - 1
    U = 8
    UW = 4
    TILES = -(-MAX_TILES // U) * U
    assert TILES <= P and TILES % (2 * U) == 0
    EPS = 1e-5
    SLOPE = 0.2
    PENALTY = -(2.0 ** 53)
    SKIP = 1 << 20
    LOWEST = -3.0e38

    ctx = ExitStack()
    with ctx:
        def sb(name, shape, dt=F32):
            return ctx.enter_context(nc.sbuf_tensor(name, shape, dt))

        def sem(name):
            return ctx.enter_context(nc.semaphore(name))

        table = nc.dram_tensor("table", (E * N, ROW), F32, kind="Internal").ap()
        result = nc.dram_tensor("result", (TOPK * N, D), F32, kind="Internal").ap()

        arena = sb("arena", [P, 12 * N + 2 * T])

        def carver(at):
            def carve(width, *dims):
                view = arena[:, at[0]:at[0] + width]
                at[0] += width
                return view
            return carve

        carve = carver([0])
        adj_r = carve(2 * N).bitcast(BF16).rearrange("p (s n) -> p s n", s=4)
        low_r = carve(2 * N).rearrange("p (s n) -> p s n", s=2)
        z_r = carve(3 * N).rearrange("p (s n) -> p s n", s=3)
        pt_r = carve(2 * T * P).rearrange("p (s t i) -> p s t i", s=2, t=T)
        trow = carve(N)
        h = carve(T * (D + 2)).rearrange("p (t d) -> p t d", t=T)
        pen = carve(N).bitcast(BF16).rearrange("p (s n) -> p s n", s=2)

        carve = carver([0])
        w1a = carve(E * W1W).rearrange("p (e w) -> p e w", e=E)
        rows_in = carve(U * ROW).rearrange("p (u w) -> p u w", u=U)
        xgT = carve(U * P).rearrange("p (u i) -> p u i", u=U)
        hT = carve(U * HB * P).rearrange("p (u b i) -> p u b i", u=U, b=HB)
        ys = carve(U * D).rearrange("p (u d) -> p u d", u=U)
        w1s = carve(UW * W1W).rearrange("p (u w) -> p u w", u=UW)
        t_rep = carve(3 * P).rearrange("p (k i) -> p k i", k=3)
        etab = carve(2 * P).bitcast(I32).rearrange("p (k i) -> p k i", k=2)
        skip = carve(P)
        crow, strow, tg, t_hot = (carve(E) for _ in range(4))
        t_junk = carve(2 * E).rearrange("p (k e) -> p k e", k=2)
        combT = arena[0:E, 2 * N:3 * N]
        zl = arena[:, 0:2 * N].rearrange("p (k t d) -> p k t d", k=TOPK, t=T)
        xh, xhT = z_r[:, 1, :].rearrange("p (t d) -> p t d", t=T), z_r[:, 2, :]

        s8 = sb("s8", [P, T])
        xs = sb("xs", [P, T, D])
        w2s = sb("w2s", [P, E, HB, D])
        store_row = sb("store_row", [P, U], I32)
        rows_out = sb("rows_out", [P, T, TOPK, ROW])
        x2T = sb("x2T", [P, GRP * P])
        a2rep, bwrep, a2w = (x2T[:, k * P:(k + 1) * P] for k in range(3))
        ident = sb("ident", [P, P])
        before = sb("before", [P, P], BF16)
        upto = sb("upto", [P, P], BF16)
        ones = sb("ones", [P, P], BF16)
        iota_e = sb("iota_e", [P, E])
        iota_i = sb("iota_i", [P, E], I32)
        pidx_i = sb("pidx_i", [P, 1], I32)
        pidx = sb("pidx", [P, 1])
        ids = sb("ids", [P, T, TOPK], I32)
        expo = sb("expo", [P, T])
        wts = sb("wts", [P, 2 * D + E + 4])
        w_s, wt_s, wr_s = wts[:, 0:D], wts[:, D:2 * D + 1], wts[:, 2 * D + 1:2 * D + 1 + E]
        a_s, bw_c = wts[:, 2 * D + 1 + E:2 * D + 3 + E], wts[:, 2 * D + 3 + E:2 * D + 4 + E]
        a_sum = sb("a_sum", [P, 1])
        bss = sb("bss", [P, D + 1 + E])
        hbias, br_s = bss[:, 0:D + 1], bss[:, D + 1:D + 1 + E]
        b2_s = sb("b2_s", [E, D])
        st = sb("st", [P, T, 6])
        mv = sb("mv", [P, T, 2])
        ve = sb("ve", [P, T])
        rstd = sb("rstd", [P, T])
        st2, mv2, ve2, rstd2 = st, mv, ve, rstd
        tmax = sb("tmax", [P, T])
        r8 = sb("r8", [P, T])
        v2 = sb("v2", [P, T])
        c_lo = sb("c_lo", [P, T])
        c_hi = sb("c_hi", [P, T])
        rinv = sb("rinv", [P, T])
        lg = sb("lg", [P, GRP, E])
        top8 = sb("top8", [P, GRP, 8])
        idx8 = sb("idx8", [P, GRP, 8], U32)
        idxf = sb("idxf", [P, GRP, TOPK])
        hot = sb("hot", [P, TOPK, 2 * GRP, E])
        both = sb("both", [P, 2 * GRP, E], BF16)
        cnt = sb("cnt", [P, COUNTED + 1, E], BF16)
        cnt_t = sb("cnt_t", [P, 2, E], BF16)
        rk = sb("rk", [P, TOPK, GRP, E])
        rank = sb("rank", [P, TOPK, GRP])
        posf = sb("posf", [P, TOPK, GRP])
        pos = sb("pos", [P, T, TOPK], I32)
        gd = sb("gd", [P, GRP])
        ge = sb("ge", [P, GRP])
        gs = sb("gs", [P, GRP])
        gate = sb("gate", [P, TOPK, 2 * GRP])
        cm = rk
        nm2 = sb("nm2", [P, T])
        comb = sb("comb", [P, T, E])
        fill = comb[:, :, :].rearrange("p t e -> p (t e)")[:, 0:ROW]
        ci = sb("ci", [E, 1], I32)
        ci2 = sb("ci2", [E, 1], I32)
        ntf = sb("ntf", [E, 1])
        ntrep = sb("ntrep", [E, P], BF16)
        t_e = sb("t_e", [P, 1])
        t_c = sb("t_c", [P, 1])
        t_s = sb("t_s", [P, 1])
        t_k = sb("t_k", [P, 1])
        t_last = sb("t_last", [P, 1])
        t_start = sb("t_start", [P, 1])
        t_ec = sb("t_ec", [P, 1])
        t_vals = sb("t_vals", [P, 3])
        bank = [ctx.enter_context(nc.psum_tensor(f"bank{i}", [P, 512], F32)) for i in range(8)]
        OB, M0, M1 = bank[4:6], bank[6], bank[7]

        d_x = [sem(f"d_x{i}") for i in range(4)]
        d_small = sem("d_small")
        d_w2 = sem("d_w2")
        d_adj = [sem(f"d_adj{i}") for i in range(4)]
        d_fill = sem("d_fill")
        d_put = sem("d_put")
        s_const = sem("s_const")
        s_pool = sem("s_pool")
        s_fill = sem("s_fill")
        s_prep = sem("s_prep")
        s_stat = sem("s_stat")
        s_rstd = sem("s_rstd")
        s_norm = sem("s_norm")
        s_xT = sem("s_xT")
        s_xTs = sem("s_xTs")
        s_wa = sem("s_wa")
        s_was = sem("s_was")
        s_tr = sem("s_tr")
        s_trs = sem("s_trs")
        s_h = sem("s_h")
        s_hs = sem("s_hs")
        s_pen = sem("s_pen")
        s_z = sem("s_z")
        s_s8 = sem("s_s8")
        s_rv = sem("s_rv")
        s_lo = sem("s_lo")
        s_hi = sem("s_hi")
        s_low = sem("s_low")
        s_lk = sem("s_lk")
        s_pt = sem("s_pt")
        s_ea = sem("s_ea")
        s_o = sem("s_o")
        s_ri = sem("s_ri")
        s_x1 = sem("s_x1")
        s_st2 = sem("s_st2")
        s_mv2 = sem("s_mv2")
        s_ve2 = sem("s_ve2")
        s_rstd2 = sem("s_rstd2")
        s_row = sem("s_row")
        s_x2t = sem("s_x2t")
        s_x2s = sem("s_x2s")
        s_lgp = sem("s_lgp")
        s_lg = sem("s_lg")
        s_dve = sem("s_dve")
        s_gd = sem("s_gd")
        s_ge = sem("s_ge")
        s_gate = sem("s_gate")
        s_both = sem("s_both")
        s_cnt = sem("s_cnt")
        s_rk = sem("s_rk")
        s_pos = sem("s_pos")
        s_comb = sem("s_comb")
        s_pl = sem("s_pl")
        s_ct = sem("s_ct")
        s_cts = sem("s_cts")
        s_b2 = sem("s_b2")
        s_base = sem("s_base")
        s_tp = sem("s_tp")
        s_tt = sem("s_tt")
        s_tab = sem("s_tab")
        e_r = [sem(f"e_r{i}") for i in range(U)]
        e_put = [sem(f"e_put{i}") for i in range(U)]
        e_xt = sem("e_xt")
        e_xts = sem("e_xts")
        e_h = sem("e_h")
        e_ha = sem("e_ha")
        e_hb = sem("e_hb")
        e_y = sem("e_y")
        e_ys = sem("e_ys")
        e_id = sem("e_id")
        d_z = [sem(f"d_z{i}") for i in range(4)]
        s_f1 = sem("s_f1")
        s_f2 = sem("s_f2")
        d_out = sem("d_out")

        d_w1 = sem("d_w1")
        s_nm2 = sem("s_nm2")
        e_wc = sem("e_wc")
        block = ctx.enter_context(nc.Block())

        def xp(u):
            return bank[u % 2][:, 0:P]

        def hp(u, b):
            return bank[2 + 2 * b + u % 2][:, 0:P]

        def yp(u):
            return bank[6 + u % 2][:, 0:D]

        def kept(q):
            return slice(SLOT[q], SLOT[q] + SIZE[q])

        def low(t):
            return low_r[:, t % 2, :]

        def numbers(engine, name):
            return [engine.alloc_register(f"{name}{u}") for u in range(U)]

        @block.sync
        def _(sp):
            xt = x.rearrange("(t p) d -> p t d", p=P)
            for c in range(4):
                sp.dma_start(xs[:, 4 * c:4 * c + 4, :], xt[:, 4 * c:4 * c + 4, :]).then_inc(d_x[c], 16)
            FILLS = 8
            padded = table.rearrange("(e n) w -> n e w", e=E)[0:P, :, :]
            for t in range(4, T):
                sp.wait_ge(s_lk, t - 3)
                if 4 <= t < 4 + FILLS:
                    e0, ne = (t - 4) * (E // FILLS), E // FILLS
                    if t == 4:
                        sp.wait_ge(s_fill, 3)
                    sp.dma_start(padded[:, e0:e0 + ne, :],
                                 fill.rearrange("p (e w) -> p e w", e=1).to_broadcast([P, ne, ROW])).then_inc(d_fill, 16)
                if t >= 12:
                    e0, ne = (t - 12) * (E // 4), E // 4
                    sp.dma_start(w2s[:, e0:e0 + ne, :, :], w2[:, e0:e0 + ne, :, :]).then_inc(d_w2, 16)

            CH = 8
            for c in range(E // CH):
                last = (c + 1) * CH * W1W
                if last <= 4 * N:
                    sp.wait_ge(s_lk, T)
                elif last <= 7 * N:
                    sp.wait_ge(s_pt, 4 * T)
                else:
                    sp.wait_ge(s_o, T)
                sp.dma_start(w1a[:, c * CH:(c + 1) * CH, :], w1b[:, c * CH:(c + 1) * CH, :]).then_inc(d_w1, 16)

            sp.wait_ge(s_tab, 3)
            first_row = numbers(sp, "first_row")
            sp.wait_ge(d_put, 16 * TOPK * T)
            sp.load(first_row, etab[0:1, 1, 0:U])
            for u in range(U):
                r = sp.snap(first_row[u], min_val=0, max_val=E * N - P)
                sp.dma_start(rows_in[:, u, :], table[bass.ds(r, P), :]).then_inc(e_r[u], 16)
            with sp.Fori(1, TILES // U) as i:
                sp.load(first_row, etab[0:1, 1, bass.ds(i * U, U)])
                for u in range(U):
                    r = sp.snap(first_row[u], min_val=0, max_val=E * N - P)
                    sp.wait_ge(e_ys, i * U + (u + 1 - U))
                    sp.wait_ge(e_id, i * U + (u + 1 - U))
                    sp.dma_start(rows_in[:, u, :], table[bass.ds(r, P), :]).then_inc(e_r[u], 16)

            for u in range(U):
                sp.wait_ge(e_put[u], 16 * (TILES // U))
            zt = result.rearrange("(k t p) d -> p k t d", k=TOPK, p=P)
            for c in range(4):
                for k in range(TOPK):
                    sp.dma_start(zl[:, k, 4 * c:4 * c + 4, :], zt[:, k, 4 * c:4 * c + 4, :]).then_inc(d_z[c], 16)
            ot = out.rearrange("(t p) d -> p t d", p=P)
            for c in range(4):
                sp.wait_ge(s_f2, c + 1)
                sp.dma_start(ot[:, 4 * c:4 * c + 4, :], xs[:, 4 * c:4 * c + 4, :]).then_inc(d_out, 16)
            sp.wait_ge(d_out, 64)

        @block.gpsimd
        def _(pool):
            def link(ins, n=[0]):
                n[0] += 1
                ins.then_inc(s_pl, 1)
                pool.wait_ge(s_pl, n[0])

            def load(t):
                if t >= 4:
                    pool.wait_ge(s_pen, t - 3)
                pool.dma_start(adj_r[:, t % 4, :], adj[t * P:(t + 1) * P, :]).then_inc(d_adj[t % 4], 16)

            pool.memset(expo[:, :], -0.5)
            link(pool.memset(ident[:, :], 0.0))
            pool.affine_select(out=ident[:, :], in_=ident[:, :], compare_op=ALU.not_equal, fill=1.0,
                               base=0, pattern=[[-1, P]], channel_multiplier=1).then_inc(s_const, 1)
            pool.memset(fill, 0.0).then_inc(s_fill, 1)
            pool.wait_ge(s_fill, 1)
            pool.memset(fill[:, ID_COL:ID_COL + 1].bitcast(I32), SKIP).then_inc(s_fill, 2)
            pool.memset(h[:, :, D + 1:D + 2], 1.0).then_inc(s_pool, 1)
            link(pool.memset(ones[:, :], 1.0))
            pool.affine_select(out=before[:, :], in_=ones[:, :], compare_op=ALU.is_gt, fill=0.0,
                               base=0, pattern=[[1, P]], channel_multiplier=-1).then_inc(s_pool, 1)
            pool.affine_select(out=upto[:, :], in_=ones[:, :], compare_op=ALU.is_ge, fill=0.0,
                               base=0, pattern=[[1, P]], channel_multiplier=-1).then_inc(s_pool, 1)
            pool.iota(iota_i[:, :], pattern=[[1, E]], base=0, channel_multiplier=0)
            pool.iota(ids[:, :, :], pattern=[[P, T], [N, TOPK]], base=0, channel_multiplier=1)
            link(pool.iota(pidx_i[:, :], pattern=[[1, 1]], base=0, channel_multiplier=1))
            pool.tensor_copy(iota_e[:, :], iota_i[:, :])
            pool.tensor_copy(pidx[:, :], pidx_i[:, :])
            pool.memset(cnt[:, 0, :], 0.0).then_inc(s_pool, 1)
            for c in range(4):
                pool.wait_ge(s_stat, c + 1)
                ct = slice(4 * c, 4 * c + 4)
                pool.tensor_tensor(rstd[:, ct], ve[:, ct], expo[:, ct], ALU.pow).then_inc(s_rstd, 1)
                load(c)

            def rstd_of(t):
                pool.wait_ge(s_mv2, t + 1)
                pool.tensor_scalar(ve2[:, t:t + 1], mv2[:, t, 1:2], EPS, None, ALU.add).then_inc(s_ve2, 1)
                pool.wait_ge(s_ve2, t + 1)
                pool.tensor_tensor(rstd2[:, t:t + 1], ve2[:, t:t + 1], expo[:, 0:1], ALU.pow).then_inc(s_rstd2, 1)
                pool.wait_ge(s_rstd2, t + 1)
                pool.tensor_scalar(nm2[:, t:t + 1], mv2[:, t, 0:1], rstd2[:, t:t + 1], -1.0, ALU.mult, ALU.mult).then_inc(s_nm2, 1)

            def counts(q):
                pool.wait_ge(s_both, q + 1)
                b = both[:, kept(q), :]
                acc = cnt[:, q, :]
                for g in range(SIZE[q] - 1):
                    link(pool.tensor_tensor(cnt_t[:, g % 2, :], acc, b[:, g, :], ALU.add))
                    acc = cnt_t[:, g % 2, :]
                pool.tensor_tensor(cnt[:, q + 1, :], acc, b[:, SIZE[q] - 1, :], ALU.add).then_inc(s_cnt, 1)

            def place(q, t):
                pool.wait_ge(s_pos, q + 1)
                for k in range(TOPK):
                    pool.indirect_dma_start(table[:, :], bass.IndirectOffsetOnAxis(pos[:, t, k:k + 1], 0),
                                            rows_out[:, t, k, :], None).then_inc(d_put, 16)

            def combine(q):
                n = SIZE[q]
                if q >= 1:
                    pool.wait_ge(s_comb, q)
                for k in range(TOPK):
                    ins = pool.tensor_tensor(cm[:, k, 0:n, :], hot[:, k, kept(q), :],
                                             gate[:, k, kept(q)].rearrange("p (g e) -> p g e", e=1).to_broadcast([P, n, E]), ALU.mult)
                link(ins)
                pool.tensor_tensor(comb[:, START[q]:START[q + 1], :], cm[:, 0, 0:n, :], cm[:, 1, 0:n, :], ALU.add).then_inc(s_comb, 1)

            load(4)
            for s in range(T + 7):
                if 0 <= s - 3 < T:
                    rstd_of(s - 3)
                if s + 5 < T:
                    load(s + 5)
                if s == START[1] + 6:
                    pool.wait_ge(d_fill, 16 * 8)
                for q in range(NG):
                    z = START[q + 1]
                    if s == z + 5 and q < COUNTED:
                        counts(q)
                    for j in range(SIZE[q]):
                        if s == z + 6 + (0 if z > T - 3 else (j + q // 2) // 2):
                            place(q, START[q] + j)
                    if q < 2 and s == z + 6:
                        combine(q)
            for q in range(2, NG):
                combine(q)

            limit = pool.alloc_register("last_result_row")
            pool.reg_mov(limit, TOPK * N - 1)
            def store(u):
                pool.indirect_dma_start(result[:, :], bass.IndirectOffsetOnAxis(store_row[:, u:u + 1], 0),
                                        ys[:, u, :], None, bounds_check=limit, oob_is_err=False).then_inc(e_put[u], 16)

            rounds = 2
            for n in range(rounds * U):
                pool.wait_ge(e_ys, n + 1)
                pool.wait_ge(e_id, n + 1)
                store(n % U)
            tile = pool.alloc_register("tiles_stored")
            pool.reg_mov(tile, rounds * U + 1)
            with pool.Fori(1, TILES // (rounds * U)) as i:
                for n in range(rounds * U):
                    pool.wait_ge(e_ys, tile)
                    pool.wait_ge(e_id, tile)
                    pool.reg_add(tile, tile, 1)
                    store(n % U)

        @block.scalar
        def _(act):
            act.dma_start(wts[:, :], weights).then_inc(d_small, 16)
            act.dma_start(bss[:, :], biases.to_broadcast([P, D + 1 + E])).then_inc(d_small, 16)
            act.dma_start(b2_s[:, :], b2).then_inc(d_small, 16)
            for b in range(4):
                act.wait_ge(s_xT, b + 1)
                act.activation(xhT[:, 512 * b:512 * b + 512], bank[b][:, :], ACT.Copy).then_inc(s_xTs, 1)
            for b in range(4):
                act.wait_ge(s_tr, b + 1)
                act.activation(trow[:, 512 * b:512 * b + 512], bank[b][:, :], ACT.Copy).then_inc(s_trs, 1)

            def scores(t):
                if t == 0:
                    act.wait_ge(s_s8, 1)
                act.wait_ge(s_z, t + 1)
                act.activation(r8[:, t:t + 1], tmax[:, t:t + 1], ACT.Relu, bias=s8[:, t:t + 1], scale=1.0 - SLOPE).then_inc(s_rv, 1)
                act.activation(v2[:, t:t + 1], tmax[:, t:t + 1], ACT.Copy, scale=-SLOPE).then_inc(s_rv, 1)
                act.wait_ge(s_rv, 2 * (t + 1))
                act.activation(c_lo[:, t:t + 1], r8[:, t:t + 1], ACT.Identity, bias=v2[:, t:t + 1], scale=-1.0).then_inc(s_lo, 1)
                act.wait_ge(s_lo, t + 1)
                act.activation(low(t), z_r[:, t % 3, :], ACT.Identity, bias=c_lo[:, t:t + 1], scale=SLOPE).then_inc(s_low, 1)
                act.activation(c_hi[:, t:t + 1], c_lo[:, t:t + 1], ACT.Identity, bias=s8[:, t:t + 1]).then_inc(s_hi, 1)

            def evac(t):
                for b in range(4):
                    act.wait_ge(s_pt, 4 * t + b + 1)
                    if t >= 2:
                        act.wait_ge(s_o, t - 1)
                    act.activation(pt_r[:, t % 2, CB * b:CB * b + CB, :].rearrange("p c i -> p (c i)"),
                                   bank[b][:, :], ACT.Exp).then_inc(s_ea, 1)

            def norm(t):
                act.wait_ge(s_nm2, t + 1)
                act.activation(rows_out[:, t, :, 0:D],
                               xs[:, t, :].rearrange("p (k d) -> p k d", k=1).to_broadcast([P, TOPK, D]),
                               ACT.Identity, bias=nm2[:, t:t + 1], scale=rstd2[:, t:t + 1]).then_inc(s_row, 1)

            def route_a(q):
                act.wait_ge(s_x2t, q + 1)
                n = SIZE[q] * P
                act.activation(x2T[:, 0:n], M0[:, 0:n], ACT.Copy).then_inc(s_x2s, 1)

            def route_b(q):
                n = SIZE[q]
                act.wait_ge(s_gd, q + 1)
                act.activation(ge[:, 0:n], gd[:, 0:n], ACT.Exp).then_inc(s_ge, 1)

            for s in range(T + 7):
                if s < T:
                    scores(s)
                if 1 <= s <= T:
                    evac(s - 1)
                if 0 <= s - 3 < T:
                    norm(s - 3)
                for q in range(NG):
                    if s == START[q + 1] + 3:
                        route_a(q)
                    if s == START[q + 1] + 5:
                        route_b(q)

            def relu(u, n):
                act.wait_ge(e_h, n)
                act.activation(hT[:, u, 0, :], hp(u, 0), ACT.Relu, bias=w1s[:, u % UW, HID:HID + 1]).then_inc(e_ha, 1)

            def weigh(u, n, stored=None):
                act.wait_ge(e_y, n)
                if stored is not None:
                    act.wait_ge(e_put[u], stored)
                act.activation(ys[:, u, :], yp(u), ACT.Copy, scale=rows_in[:, u, GATE_COL:GATE_COL + 1]).then_inc(e_ys, 1)

            relu(0, 1)
            for u in range(U):
                relu((u + 1) % U, u + 2)
                weigh(u, u + 1)
            with act.Fori(1, TILES // U - 1) as i:
                for u in range(U):
                    relu((u + 1) % U, i * U + (u + 2))
                    weigh(u, i * U + (u + 1), i * 16)
            for u in range(U):
                if u < U - 1:
                    relu(u + 1, TILES - U + u + 2)
                weigh(u, TILES - U + u + 1, 16 * (TILES // U - 1))

            for q in range(NG):
                act.wait_ge(s_ct, q + 1)
                act.activation(combT[:, START[q] * P:START[q + 1] * P], bank[q][0:E, 0:SIZE[q] * P], ACT.Copy).then_inc(s_cts, 1)

        @block.vector
        def _(dve):
            chain = [0]

            def link(ins):
                chain[0] += 1
                ins.then_inc(s_dve, 1)
                dve.wait_ge(s_dve, chain[0])

            def stats(c):
                dve.wait_ge(d_x[c], 16)
                for t in range(4 * c, 4 * c + 4):
                    ins = dve.bn_stats(st[:, t, :], xs[:, t, :])
                link(ins)
                for t in range(4 * c, 4 * c + 4):
                    ins = dve.bn_aggr(mv[:, t, :], st[:, t, :])
                link(ins)
                dve.tensor_scalar(ve[:, 4 * c:4 * c + 4], mv[:, 4 * c:4 * c + 4, 1], EPS, None, ALU.add).then_inc(s_stat, 1)

            def scale(c):
                dve.wait_ge(s_rstd, c + 1)
                for t in range(4 * c, 4 * c + 4):
                    ins = dve.tensor_scalar(xh[:, t, :], xs[:, t, :], mv[:, t, 0:1], rstd[:, t:t + 1], ALU.subtract, ALU.mult)
                ins.then_inc(s_norm, 1)

            def h_evac(c):
                dve.wait_ge(s_h, c + 1)
                dve.tensor_tensor(h[:, 2 * c:2 * c + 2, 0:D + 1],
                                  bank[4 + c % 4][:, 0:2 * (D + 1)].rearrange("p (t d) -> p t d", t=2),
                                  hbias[:, :].rearrange("p (t d) -> p t d", t=1).to_broadcast([P, 2, D + 1]),
                                  ALU.add).then_inc(s_hs, 1)

            stats(0)
            stats(1)
            dve.wait_ge(d_small, 16 * 3)
            dve.tensor_copy(a2rep[:, :], a_s[:, 1:2].to_broadcast([P, P]))
            dve.tensor_copy(bwrep[:, :], bw_c[:, 0:1].to_broadcast([P, P]))
            dve.tensor_tensor(a_sum[:, :], a_s[:, 0:1], a_s[:, 1:2], ALU.add).then_inc(s_prep, 1)
            scale(0)
            stats(2)
            scale(1)
            stats(3)
            dve.wait_ge(s_wa, 1)
            dve.tensor_copy(a2w[:, :], bank[4][:, 0:P])
            dve.tensor_copy(wt_s[:, D:D + 1], bank[5][:, 0:1])
            dve.tensor_tensor(hbias[:, D:D + 1], bank[6][:, 0:1], hbias[:, D:D + 1], ALU.add).then_inc(s_was, 1)
            def penalty(t):
                dve.wait_ge(d_adj[t % 4], 16 * (t // 4 + 1))
                if t >= 2:
                    dve.wait_ge(s_z, t - 1)
                dve.tensor_scalar(pen[:, t % 2, :], adj_r[:, t % 4, :], 0, PENALTY, ALU.is_le, ALU.mult).then_inc(s_pen, 1)

            def scores(t):
                if t == 0:
                    dve.wait_ge(s_trs, 4)
                if t >= 3:
                    dve.wait_ge(s_pt, 4 * (t - 2))
                dve.wait_ge(s_pen, t + 1)
                dve.tensor_tensor_reduce(out=z_r[:, t % 3, :], in0=pen[:, t % 2, :], in1=trow[:, :], scale=1.0,
                                         scalar=LOWEST, op0=ALU.add, op1=ALU.max, accum_out=tmax[:, t:t + 1]).then_inc(s_z, 1)

            def leaky(t):
                dve.wait_ge(s_low, t + 1)
                dve.wait_ge(s_hi, t + 1)
                z = z_r[:, t % 3, :]
                dve.scalar_tensor_tensor(z, z, c_hi[:, t:t + 1], low(t), ALU.add, ALU.max).then_inc(s_lk, 1)

            def residual(t):
                dve.wait_ge(s_o, t + 1)
                dve.reciprocal(rinv[:, t:t + 1], OB[t % 2][:, D + 1:D + 2]).then_inc(s_ri, 1)
                dve.wait_ge(s_ri, t + 1)
                dve.scalar_tensor_tensor(xs[:, t, :], OB[t % 2][:, 0:D], rinv[:, t:t + 1], xs[:, t, :],
                                         ALU.mult, ALU.add).then_inc(s_x1, 1)
                dve.wait_ge(s_x1, t + 1)
                dve.bn_stats(st2[:, t, :], xs[:, t, :]).then_inc(s_st2, 1)
                dve.wait_ge(s_st2, t + 1)
                dve.bn_aggr(mv2[:, t, :], st2[:, t, :]).then_inc(s_mv2, 1)

            def top2(q):
                n = SIZE[q]
                dve.wait_ge(s_lgp, q + 1)
                dve.tensor_tensor(lg[:, 0:n, :], M0[:, 0:n * E].rearrange("p (g e) -> p g e", g=n),
                                  br_s[:, :].rearrange("p (g e) -> p g e", g=1).to_broadcast([P, n, E]), ALU.add).then_inc(s_lg, 1)
                dve.wait_ge(s_lg, q + 1)
                for g in range(n):
                    ins = dve.max(top8[:, g, :], lg[:, g, :])
                link(ins)
                dve.tensor_tensor(gd[:, 0:n], top8[:, 0:n, 1], top8[:, 0:n, 0], ALU.subtract).then_inc(s_gd, 1)
                for g in range(n):
                    ins = dve.max_index(idx8[:, g, :], top8[:, g, :], lg[:, g, :])
                link(ins)
                link(dve.tensor_copy(idxf[:, 0:n, :], idx8[:, 0:n, 0:TOPK]))
                if q >= 2:
                    dve.wait_ge(s_comb, min(q - 1, 2))
                for k in range(TOPK):
                    ins = dve.tensor_tensor(hot[:, k, kept(q), :],
                                            iota_e[:, :].rearrange("p (g e) -> p g e", g=1).to_broadcast([P, n, E]),
                                            idxf[:, 0:n, k:k + 1].to_broadcast([P, n, E]), ALU.is_equal)
                link(ins)
                dve.tensor_tensor(both[:, kept(q), :], hot[:, 0, kept(q), :], hot[:, 1, kept(q), :], ALU.add).then_inc(s_both, 1)

            def place(q):
                n = SIZE[q]
                rows = slice(START[q], START[q + 1])
                dve.wait_ge(s_ge, q + 1)
                link(dve.tensor_scalar(gs[:, 0:n], ge[:, 0:n], 1.0, None, ALU.add))
                link(dve.reciprocal(gate[:, 0, kept(q)], gs[:, 0:n]))
                dve.tensor_tensor(gate[:, 1, kept(q)], ge[:, 0:n], gate[:, 0, kept(q)], ALU.mult).then_inc(s_gate, 1)
                dve.wait_ge(s_rk, q + 1)
                if 1 <= q <= 2:
                    dve.wait_ge(s_comb, q)
                for k in range(TOPK):
                    ins = dve.tensor_tensor(rk[:, k, 0:n, :], M1[:, 0:n * E].rearrange("p (g e) -> p g e", g=n),
                                            hot[:, k, kept(q), :], ALU.mult)
                link(ins)
                link(dve.tensor_reduce(rank[:, :, 0:n], rk[:, :, 0:n, :], AX.X, ALU.add))
                link(dve.scalar_tensor_tensor(posf[:, :, 0:n], idxf[:, 0:n, :].rearrange("p g k -> p k g"), float(N),
                                              rank[:, :, 0:n], ALU.mult, ALU.add))
                dve.wait_ge(s_gate, q + 1)
                dve.tensor_copy(rows_out[:, rows, :, ID_COL].bitcast(I32), ids[:, rows, :])
                dve.tensor_copy(rows_out[:, rows, :, GATE_COL], gate[:, :, kept(q)].rearrange("p k g -> p g k"))
                dve.tensor_copy(pos[:, rows, :].rearrange("p g k -> p k g"), posf[:, :, 0:n]).then_inc(s_pos, 1)

            def base(q):
                dve.wait_ge(s_b2, q + 1)
                xq = xs[:, START[q]:START[q + 1], :].rearrange("p g d -> p (g d)")
                dve.tensor_tensor(xq, xq, bank[q][:, 0:SIZE[q] * P], ALU.add).then_inc(s_base, 1)

            scale(2)
            h_evac(0)
            h_evac(1)
            scale(3)
            h_evac(2)
            h_evac(3)
            penalty(0)
            penalty(1)
            for c in range(4, 8):
                h_evac(c)
            dve.wait_ge(s_hs, 8)
            dve.tensor_scalar(s8[:, :], h[:, :, D], 1.0 - SLOPE, None, ALU.mult).then_inc(s_s8, 1)
            scores(0)
            dve.wait_ge(s_pool, 4)
            for s in range(1, T + 7):
                if s < T:
                    scores(s)
                if s + 1 < T:
                    penalty(s + 1)
                if 1 <= s <= T:
                    leaky(s - 1)
                if 0 <= s - 3 < T:
                    residual(s - 3)
                for q in range(NG):
                    if s == START[q + 1] + 5:
                        top2(q)
                    if s == START[q + 1] + 6:
                        place(q)

            dve.wait_ge(s_tp, 1)
            link(dve.tensor_scalar(ci[:, :], M0[0:E, 0:1], float(P - 1), None, ALU.add))
            dve.tensor_copy(crow[:, :], M0[:, E:2 * E])
            link(dve.tensor_scalar(ci2[:, :], ci[:, :], P.bit_length() - 1, None, ALU.arith_shift_right))
            link(dve.tensor_copy(ntf[:, :], ci2[:, :]))
            dve.tensor_copy(ntrep[:, :], ntf[:, :].to_broadcast([E, P])).then_inc(s_tt, 1)
            dve.wait_ge(s_tp, 2)
            link(dve.tensor_copy(strow[:, :], M0[:, 3 * E:4 * E]))
            link(dve.tensor_scalar(tg[:, :], M0[:, 2 * E:3 * E], pidx[:, :], None, ALU.is_le))
            link(dve.tensor_reduce(t_e[:, :], tg[:, :], AX.X, ALU.add))
            link(dve.tensor_scalar(t_hot[:, :], iota_e[:, :], t_e[:, :], None, ALU.is_equal))
            dve.tensor_tensor(t_junk[:, 0, :], t_hot[:, :], crow[:, :], ALU.mult)
            link(dve.tensor_tensor(t_junk[:, 1, :], t_hot[:, :], strow[:, :], ALU.mult))
            dve.tensor_reduce(t_c[:, :], t_junk[:, 0, :], AX.X, ALU.add)
            link(dve.tensor_reduce(t_s[:, :], t_junk[:, 1, :], AX.X, ALU.add))
            dve.tensor_scalar(t_last[:, :], t_c[:, :], float(-P), 0.0, ALU.add, ALU.max)
            link(dve.tensor_tensor(t_k[:, :], pidx[:, :], t_s[:, :], ALU.subtract))
            link(dve.tensor_scalar(t_k[:, :], t_k[:, :], float(P), None, ALU.mult))
            dve.tensor_scalar(t_ec[:, :], t_e[:, :], float(E - 1), None, ALU.min)
            link(dve.tensor_tensor(t_start[:, :], t_k[:, :], t_last[:, :], ALU.min))
            dve.tensor_copy(t_vals[:, 0:1], t_ec[:, :])
            dve.scalar_tensor_tensor(t_vals[:, 1:2], t_ec[:, :], float(N), t_start[:, :], ALU.mult, ALU.add)
            link(dve.tensor_tensor(t_vals[:, 2:3], t_k[:, :], t_start[:, :], ALU.subtract))
            dve.tensor_copy(t_rep[:, :, :], t_vals[:, :].rearrange("p (k o) -> p k o", o=1).to_broadcast([P, 3, P])).then_inc(s_tt, 1)
            dve.wait_ge(s_tp, 3)
            dve.tensor_copy(etab[:, :, :], M0[:, 0:2 * P].rearrange("p (k o) -> p k o", k=2)).then_inc(s_tab, 1)
            dve.tensor_scalar(skip[:, :], M0[:, 2 * P:3 * P], pidx[:, :], float(SKIP), ALU.is_gt, ALU.mult).then_inc(s_tab, 2)

            def take(u, n, t, e, stored=None):
                dve.wait_ge(e_xt, n)
                dve.tensor_copy(xgT[:, u, :], xp(u)).then_inc(e_xts, 1)
                e = dve.snap(e, min_val=0, max_val=E - 1)
                dve.tensor_copy(w1s[:, u % UW, :], w1a[:, bass.ds(e, 1), :].rearrange("p e w -> p (e w)")).then_inc(e_wc, 1)
                if stored is not None:
                    dve.wait_ge(e_put[u], stored)
                dve.tensor_tensor(store_row[:, u:u + 1], rows_in[:, u, ID_COL:ID_COL + 1].bitcast(I32), skip[:, t],
                                  ALU.add).then_inc(e_id, 1)

            def relu(u, n):
                dve.wait_ge(e_h, n)
                dve.tensor_scalar(hT[:, u, 1, :], hp(u, 1), w1s[:, u % UW, HID + 1:HID + 2], 0.0, ALU.add, ALU.max).then_inc(e_hb, 1)

            dve.wait_ge(s_tab, 3)
            dve.wait_ge(d_w1, 16 * (E // 8))
            expert = numbers(dve, "expert")
            dve.load(expert, etab[0:1, 0, 0:U])
            for u in range(U):
                take(u, u + 1, slice(u, u + 1), expert[u])
                if u:
                    relu(u - 1, u)
            with dve.Fori(1, TILES // U) as i:
                dve.load(expert, etab[0:1, 0, bass.ds(i * U, U)])
                for u in range(U):
                    take(u, i * U + (u + 1), bass.ds(i * U + u, 1), expert[u], i * 16)
                    relu((u - 1) % U, i * U + u)
            relu(U - 1, TILES)

            for q in range(NG):
                base(q)
            for c in range(4):
                dve.wait_ge(d_z[c], 32)
                if c == 0:
                    dve.wait_ge(s_base, NG)
                xc = xs[:, 4 * c:4 * c + 4, :]
                dve.tensor_tensor(xc, xc, zl[:, 0, 4 * c:4 * c + 4, :], ALU.add).then_inc(s_f1, 1)
                dve.wait_ge(s_f1, c + 1)
                dve.tensor_tensor(xc, xc, zl[:, 1, 4 * c:4 * c + 4, :], ALU.add).then_inc(s_f2, 1)

        @block.tensor
        def _(pe):
            pe.wait_ge(s_prep, 1)
            pe.matmul(bank[4][:, 0:P], w_s[:, :], a2rep[:, :], start=True, stop=True)
            pe.matmul(bank[5][:, 0:1], w_s[:, :], a_s[:, 0:1], start=True, stop=True)
            pe.matmul(bank[6][:, 0:1], bwrep[:, :], a_sum[:, :], start=True, stop=True).then_inc(s_wa, 1)
            pe.wait_ge(s_const, 1)

            def turn_x(b):
                pe.wait_ge(s_norm, b + 1)
                for c in range(CB):
                    ins = pe.transpose(bank[b][:, P * c:P * c + P], xh[:, CB * b + c, :], ident[:, :])
                ins.then_inc(s_xT, 1)

            def scores_row(b):
                pe.wait_ge(s_xTs, b + 1)
                pe.matmul(bank[b][:, :], a2w[:, :], xhT[:, 512 * b:512 * b + 512], start=True, stop=True).then_inc(s_tr, 1)

            def project(b):
                pe.wait_ge(s_xTs, b + 1)
                for c in (2 * b, 2 * b + 1):
                    if c >= 4:
                        pe.wait_ge(s_hs, c - 3)
                    for j in range(2):
                        t = 2 * c + j
                        ins = pe.matmul(bank[4 + c % 4][:, j * (D + 1):(j + 1) * (D + 1)], xhT[:, P * t:P * t + P],
                                        wt_s[:, :], start=True, stop=True)
                    ins.then_inc(s_h, 1)

            turn_x(0)
            turn_x(1)
            pe.wait_ge(s_was, 1)
            project(0)
            turn_x(2)
            project(1)
            turn_x(3)
            project(2)
            scores_row(0)
            project(3)
            scores_row(1)
            scores_row(2)
            scores_row(3)

            def turn(t):
                pe.wait_ge(s_lk, t + 1)
                for b in range(4):
                    if t == 0:
                        pe.wait_ge(s_trs, b + 1)
                    else:
                        pe.wait_ge(s_ea, 4 * (t - 1) + b + 1)
                    for c in range(CB):
                        j = CB * b + c
                        ins = pe.transpose(bank[b][:, P * c:P * c + P], z_r[:, t % 3, P * j:P * j + P], ident[:, :])
                    ins.then_inc(s_pt, 1)

            def attend(t):
                if t >= 2:
                    pe.wait_ge(s_x1, t - 1)
                for j in range(T):
                    b = j // CB
                    if j % CB == 0:
                        pe.wait_ge(s_ea, 4 * t + b + 1)
                    ins = pe.matmul(OB[t % 2][:, 0:D + 2], pt_r[:, t % 2, j, :], h[:, j, :], start=(j == 0), stop=(j == T - 1))
                ins.then_inc(s_o, 1)

            def route_a(q):
                pe.wait_ge(s_row, START[q + 1])
                if q >= 1:
                    pe.wait_ge(s_lg, q)
                for g in range(SIZE[q]):
                    ins = pe.transpose(M0[:, P * g:P * g + P], rows_out[:, START[q] + g, 0, 0:D], ident[:, :])
                ins.then_inc(s_x2t, 1)

            def route_b(q):
                pe.wait_ge(s_x2s, q + 1)
                for g in range(SIZE[q]):
                    ins = pe.matmul(M0[:, E * g:E * g + E], x2T[:, P * g:P * g + P], wr_s[:, :], start=True, stop=True)
                ins.then_inc(s_lgp, 1)

            def earlier(q):
                c = min(q, COUNTED)
                return [cnt[:, c, :]] + [both[:, SLOT[p] + j, :] for p in range(c, q) for j in range(SIZE[p])]

            def route_c(q):
                pe.wait_ge(s_both, q + 1)
                if q >= 1:
                    pe.wait_ge(s_cnt, min(q, COUNTED))
                    pe.wait_ge(s_pos, q)
                for g in range(SIZE[q]):
                    rows = [(before, both[:, SLOT[q] + g, :])]
                    rows += [(ones, c) for c in earlier(q)]
                    rows += [(ones, both[:, SLOT[q] + j, :]) for j in range(g)]
                    for n, (lt, r) in enumerate(rows):
                        ins = pe.matmul(M1[:, E * g:E * g + E], lt[:, :], r, start=(n == 0), stop=(n == len(rows) - 1))
                ins.then_inc(s_rk, 1)

            for s in range(T + 7):
                if s < T:
                    turn(s)
                if 1 <= s <= T:
                    attend(s - 1)
                for q in range(NG):
                    if s == START[q + 1] + 2:
                        route_a(q)
                    if s == START[q + 1] + 3:
                        route_b(q)
                for q in range(NG):
                    if s == START[q + 1] + 4:
                        route_c(q)

            total = earlier(NG)
            for n, c in enumerate(total):
                pe.matmul(M0[0:E, 0:1], c, ones[:, 0:1], start=(n == 0), stop=(n == len(total) - 1))
            for n, c in enumerate(total):
                ins = pe.matmul(M0[:, E:2 * E], ones[:, :], c, start=(n == 0), stop=(n == len(total) - 1))
            ins.then_inc(s_tp, 1)
            pe.wait_ge(s_tt, 1)
            pe.matmul(M0[:, 2 * E:3 * E], ntrep[:, :], upto[0:E, 0:E], start=True, stop=True)
            pe.matmul(M0[:, 3 * E:4 * E], ntrep[:, :], before[0:E, 0:E], start=True, stop=True).then_inc(s_tp, 1)
            pe.wait_ge(s_tt, 2)
            for k in range(3):
                ins = pe.matmul(M0[:, P * k:P * k + P], t_rep[:, k, :], ident[:, :], start=True, stop=True)
            ins.then_inc(s_tp, 1)

            def take(u, w):
                pe.wait_ge(e_r[u], w)
                pe.transpose(xp(u), rows_in[:, u, 0:D], ident[:, :]).then_inc(e_xt, 1)

            def up(u, n):
                pe.wait_ge(e_wc, n)
                for b in range(HB):
                    ins = pe.matmul(hp(u, b), w1s[:, u % UW, P * b:P * b + P], xgT[:, u, :], start=True, stop=True)
                ins.then_inc(e_h, 1)

            def down(u, n, e):
                e = pe.snap(e, min_val=0, max_val=E - 1)
                pe.wait_ge(e_ha, n)
                pe.wait_ge(e_hb, n)
                for b in range(HB):
                    ins = pe.matmul(yp(u), hT[:, u, b, :], w2s[:, bass.ds(e, 1), b, :].rearrange("p e d -> p (e d)"),
                                    start=(b == 0), stop=(b == HB - 1))
                ins.then_inc(e_y, 1)

            pe.wait_ge(d_w2, 16 * 4)
            pe.wait_ge(s_tab, 3)
            expert = numbers(pe, "expert")
            take(0, 16)
            take(1, 16)
            up(0, 1)
            more = numbers(pe, "expert_of_second_round")
            pe.load(expert, etab[0:1, 0, 0:U])
            for u in range(U):
                take((u + 2) % U, 16 if u + 2 < U else 32)
                up((u + 1) % U, u + 2)
                down(u, u + 1, expert[u])
            with pe.Fori(0, (TILES // U - 2) // 2) as i:
                pe.load(expert, etab[0:1, 0, bass.ds(i * 2 * U + U, U)])
                for n in range(2 * U):
                    if n == U:
                        pe.load(more, etab[0:1, 0, bass.ds(i * 2 * U + 2 * U, U)])
                    take((n + 2) % U, i * 32 + (32 + 16 * ((n + 2) // U)))
                    up((n + 1) % U, i * 2 * U + (U + n + 2))
                    down(n % U, i * 2 * U + (U + n + 1), expert[n] if n < U else more[n - U])
            pe.load(expert, etab[0:1, 0, TILES - U:TILES])
            for u in range(U):
                if u + 2 < U:
                    take(u + 2, 16 * (TILES // U))
                if u + 1 < U:
                    up(u + 1, TILES - U + u + 2)
                down(u, TILES - U + u + 1, expert[u])

            pe.wait_ge(e_ys, TILES)
            for q in range(NG):
                pe.wait_ge(s_comb, q + 1)
                for g in range(SIZE[q]):
                    ins = pe.transpose(bank[q][0:E, P * g:P * g + P], comb[:, START[q] + g, :], ident[:, :])
                ins.then_inc(s_ct, 1)
            for q in range(NG):
                pe.wait_ge(s_cts, q + 1)
                for g in range(SIZE[q]):
                    t = START[q] + g
                    ins = pe.matmul(bank[q][:, P * g:P * g + P], combT[:, P * t:P * t + P], b2_s[:, :], start=True, stop=True)
                ins.then_inc(s_b2, 1)


def kernel(**inputs):
    import numpy as np
    import concourse.bacc as bacc
    from concourse.bass_utils import run_bass_kernel_spmd

    a = {k: np.asarray(v) for k, v in inputs.items()}
    e, d, hid = a["L0_ffn_W1"].shape
    b1 = a["L0_ffn_b1"].reshape(e, hid // 128, 128).transpose(0, 2, 1)
    w, av = a["L0_gnn_W"], a["L0_gnn_a_vec"].reshape(2, d)
    arrays = {
        "x": a["x"],
        "adj": a["adj"],
        "weights": np.concatenate([w, w.T, np.zeros((d, 1), w.dtype), a["L0_ffn_Wr"], av.T, a["L0_gnn_b_W"][:, None]], axis=1),
        "biases": np.concatenate([a["L0_gnn_b_W"], a["L0_gnn_b_a"], a["L0_ffn_br"]])[None, :],
        "w1b": np.concatenate([a["L0_ffn_W1"], b1], axis=2).transpose(1, 0, 2),
        "w2": a["L0_ffn_W2"].reshape(e, hid // 128, 128, d).transpose(2, 0, 1, 3),
        "b2": a["L0_ffn_b2"],
    }
    arrays = {k: np.ascontiguousarray(v) for k, v in arrays.items()}
    nc = bacc.Bacc("TRN2", target_bir_lowering=False, num_devices=1)
    aps = [nc.dram_tensor(f"in_{k}", v.shape, mybir.dt.from_np(v.dtype), kind="ExternalInput").ap() for k, v in arrays.items()]
    out = nc.dram_tensor("out", a["x"].shape, mybir.dt.float32, kind="ExternalOutput").ap()
    build(nc, *aps, out)
    r = run_bass_kernel_spmd(nc, [{f"in_{k}": v for k, v in arrays.items()}], core_ids=[0])
    return r.results[0]["out"]
```
